# Optimizing a Trainium2 kernel written in Bass

```python
import numpy as np
import jax
import jax.numpy as jnp

def _softmax(x, axis=-1):
    return jax.nn.softmax(x, axis=axis)

def _gelu(x):
    return jax.nn.gelu(x, approximate=True)

def _silu(x):
    return jax.nn.silu(x)

def _sigmoid(x):
    return jax.nn.sigmoid(x)

def _layernorm(x, axis=-1, eps=1e-05):
    m = jnp.mean(x, axis=axis, keepdims=True)
    v = jnp.var(x, axis=axis, keepdims=True)
    return (x - m) / jnp.sqrt(v + eps)

def _scatter_add(tgt, idx, src, axis=0):
    return tgt.at[idx].add(src)

def _segment_sum(src, seg, n):
    return jax.ops.segment_sum(src, seg, n)
kernel_name = 'mk_sandwich_d1_jaxref_r8_dc7ed8'

def setup_inputs(seed: int=0):
    np.random.seed(seed)
    _w = jnp.asarray

    def _L0_attn_setup():
        import jax, jax.numpy as jnp
        import numpy as np
        B, S, HID = (4, 128, 128)
        H = 8
        HD = HID // H
        NQ = 8
        RATIO = 0.5
        FF = 4 * HID
        EPS_COS = 1e-08
        LN_EPS = 1e-05

        def _layernorm(x, g, b):
            m = jnp.mean(x, axis=-1, keepdims=True)
            v = jnp.var(x, axis=-1, keepdims=True)
            return (x - m) * jax.lax.rsqrt(v + LN_EPS) * g + b
        key = jax.random.key(seed)
        ks = jax.random.split(key, 24)
        sc = 0.02
        inp = {'x': jax.random.normal(ks[0], (B, S, HID), jnp.float32), 'Wq': jax.random.normal(ks[1], (H, HID, HD)) * sc, 'bq': jnp.zeros((H, HD)), 'Wk': jax.random.normal(ks[2], (H, HID, HD)) * sc, 'bk': jnp.zeros((H, HD)), 'Wv': jax.random.normal(ks[3], (H, HID, HD)) * sc, 'bv': jnp.zeros((H, HD)), 'Wc2q': jax.random.normal(ks[4], (H, HD, NQ)) * sc, 'bc2q': jnp.zeros((H, NQ)), 'Wo': jax.random.normal(ks[5], (HID, HID)) * sc, 'bo': jnp.zeros((HID,)), 'g1': jnp.ones((HID,)), 'beta1': jnp.zeros((HID,)), 'g2': jnp.ones((HID,)), 'beta2': jnp.zeros((HID,)), 'W1': jax.random.normal(ks[6], (HID, FF)) * sc, 'b1': jnp.zeros((FF,)), 'Wm': jax.random.normal(ks[7], (FF, NQ)) * sc, 'bm': jnp.zeros((NQ,)), 'Wqo': jax.random.normal(ks[8], (NQ, FF)) * sc, 'bqo': jnp.zeros((FF,)), 'W2': jax.random.normal(ks[9], (FF, HID)) * sc, 'b2': jnp.zeros((HID,))}
        return inp
    _L0_attn_in = _L0_attn_setup()

    def _L0_ffn_setup():
        import jax, jax.numpy as jnp
        import numpy as np
        NUM_EXPERTS = 8
        N_EMBD = 128
        D_FF = 4 * N_EMBD
        B, S = (4, 256)
        key = jax.random.key(seed)
        ks = jax.random.split(key, 6)
        x = jax.random.normal(ks[0], (B, S, N_EMBD), dtype=jnp.float32)
        gate_w = jax.random.normal(ks[1], (N_EMBD, NUM_EXPERTS), dtype=jnp.float32) * 0.02
        w1 = jax.random.normal(ks[2], (NUM_EXPERTS, N_EMBD, D_FF), dtype=jnp.float32) * 0.02
        b1 = jnp.zeros((NUM_EXPERTS, D_FF), dtype=jnp.float32)
        w2 = jax.random.normal(ks[3], (NUM_EXPERTS, D_FF, N_EMBD), dtype=jnp.float32) * 0.02
        b2 = jnp.zeros((NUM_EXPERTS, N_EMBD), dtype=jnp.float32)
        return {'x': x, 'gate_w': gate_w, 'w1': w1, 'b1': b1, 'w2': w2, 'b2': b2}
    _L0_ffn_in = _L0_ffn_setup()
    _d = {'L0_attn_x': _L0_attn_in['x'], 'L0_attn_Wq': _L0_attn_in['Wq'], 'L0_attn_bq': _L0_attn_in['bq'], 'L0_attn_Wk': _L0_attn_in['Wk'], 'L0_attn_bk': _L0_attn_in['bk'], 'L0_attn_Wv': _L0_attn_in['Wv'], 'L0_attn_bv': _L0_attn_in['bv'], 'L0_attn_Wc2q': _L0_attn_in['Wc2q'], 'L0_attn_bc2q': _L0_attn_in['bc2q'], 'L0_attn_Wo': _L0_attn_in['Wo'], 'L0_attn_bo': _L0_attn_in['bo'], 'L0_attn_g1': _L0_attn_in['g1'], 'L0_attn_beta1': _L0_attn_in['beta1'], 'L0_attn_g2': _L0_attn_in['g2'], 'L0_attn_beta2': _L0_attn_in['beta2'], 'L0_attn_W1': _L0_attn_in['W1'], 'L0_attn_b1': _L0_attn_in['b1'], 'L0_attn_Wm': _L0_attn_in['Wm'], 'L0_attn_bm': _L0_attn_in['bm'], 'L0_attn_Wqo': _L0_attn_in['Wqo'], 'L0_attn_bqo': _L0_attn_in['bqo'], 'L0_attn_W2': _L0_attn_in['W2'], 'L0_attn_b2': _L0_attn_in['b2'], 'L0_ffn_gate_w': _L0_ffn_in['gate_w'], 'L0_ffn_w1': _L0_ffn_in['w1'], 'L0_ffn_b1': _L0_ffn_in['b1'], 'L0_ffn_w2': _L0_ffn_in['w2'], 'L0_ffn_b2': _L0_ffn_in['b2']}
    _x0 = _d['L0_attn_x']
    _d['L0_attn_x'] = jax.random.normal(jax.random.fold_in(jax.random.key(seed), 1), (16, 256, 128), dtype=_x0.dtype)
    del _x0
    return _d

def reference(L0_attn_x, L0_attn_Wq, L0_attn_bq, L0_attn_Wk, L0_attn_bk, L0_attn_Wv, L0_attn_bv, L0_attn_Wc2q, L0_attn_bc2q, L0_attn_Wo, L0_attn_bo, L0_attn_g1, L0_attn_beta1, L0_attn_g2, L0_attn_beta2, L0_attn_W1, L0_attn_b1, L0_attn_Wm, L0_attn_bm, L0_attn_Wqo, L0_attn_bqo, L0_attn_W2, L0_attn_b2, L0_ffn_gate_w, L0_ffn_w1, L0_ffn_b1, L0_ffn_w2, L0_ffn_b2):

    def _L0_attn_ref(x, Wq, bq, Wk, bk, Wv, bv, Wc2q, bc2q, Wo, bo, g1, beta1, g2, beta2, W1, b1, Wm, bm, Wqo, bqo, W2, b2):
        import jax, jax.numpy as jnp
        import numpy as np
        B, S, HID = (4, 128, 128)
        H = 8
        HD = HID // H
        NQ = 8
        RATIO = 0.5
        FF = 4 * HID
        EPS_COS = 1e-08
        LN_EPS = 1e-05

        def _layernorm(x, g, b):
            m = jnp.mean(x, axis=-1, keepdims=True)
            v = jnp.var(x, axis=-1, keepdims=True)
            return (x - m) * jax.lax.rsqrt(v + LN_EPS) * g + b
        Q = jnp.einsum('bsh,nhd->bnsd', x, Wq) + bq[None, :, None, :]
        K = jnp.einsum('bsh,nhd->bnsd', x, Wk) + bk[None, :, None, :]
        V = jnp.einsum('bsh,nhd->bnsd', x, Wv) + bv[None, :, None, :]
        qq = jnp.einsum('bnsd,ndq->bnsq', Q, Wc2q) + bc2q[None, :, None, :]
        kq = jnp.einsum('bnsd,ndq->bnsq', K, Wc2q) + bc2q[None, :, None, :]
        qn = jnp.linalg.norm(qq, axis=-1)
        kn = jnp.linalg.norm(kq, axis=-1)
        dots = jnp.einsum('bnsq,bntq->bnst', qq, kq)
        fid = dots / jnp.maximum(qn[..., :, None] * kn[..., None, :], EPS_COS)
        qw = fid * (1.0 + 0.1 * jnp.sin(fid * jnp.pi))
        cw = jnp.einsum('bnsd,bntd->bnst', Q, K) / np.sqrt(HD).astype(np.float32)
        aw = RATIO * qw + (1.0 - RATIO) * cw
        probs = jax.nn.softmax(aw, axis=-1)
        heads = jnp.einsum('bnst,bntd->bnsd', probs, V)
        attn = heads.transpose(0, 2, 1, 3).reshape(x.shape[0], x.shape[1], HID)
        attn = attn @ Wo + bo
        x1 = _layernorm(x + attn, g1, beta1)
        h = x1 @ W1 + b1
        qm = h @ Wm + bm
        qe = jnp.tanh(qm) * jnp.cos(qm * (jnp.pi / 4))
        ha = qe @ Wqo + bqo
        ff = ha @ W2 + b2
        out = _layernorm(x1 + ff, g2, beta2)
        return out

    def _L0_ffn_ref(x, gate_w, w1, b1, w2, b2):
        import jax, jax.numpy as jnp
        import numpy as np
        NUM_EXPERTS = 8
        N_EMBD = 128
        D_FF = 4 * N_EMBD
        B, S = (4, 256)
        Bb, Ss, D = x.shape
        x_flat = x.reshape(-1, D)
        router_logits = x_flat @ gate_w
        router_probs = jax.nn.softmax(router_logits, axis=-1)
        expert_idx = jnp.argmax(router_probs, axis=-1)
        expert_w = jnp.take_along_axis(router_probs, expert_idx[:, None], axis=1)[:, 0]
        out = jnp.zeros_like(x_flat)
        for e in range(NUM_EXPERTS):
            h = jax.nn.gelu(x_flat @ w1[e] + b1[e], approximate=False)
            y = h @ w2[e] + b2[e]
            sel = expert_idx == e
            out = out + jnp.where(sel, expert_w, 0.0)[:, None] * y
        return out.reshape(Bb, Ss, D)
    x = L0_attn_x
    x = x + _layernorm(_L0_attn_ref(_layernorm(x, axis=-1), L0_attn_Wq, L0_attn_bq, L0_attn_Wk, L0_attn_bk, L0_attn_Wv, L0_attn_bv, L0_attn_Wc2q, L0_attn_bc2q, L0_attn_Wo, L0_attn_bo, L0_attn_g1, L0_attn_beta1, L0_attn_g2, L0_attn_beta2, L0_attn_W1, L0_attn_b1, L0_attn_Wm, L0_attn_bm, L0_attn_Wqo, L0_attn_bqo, L0_attn_W2, L0_attn_b2), axis=-1)
    x = x + _layernorm(_L0_ffn_ref(_layernorm(x, axis=-1), L0_ffn_gate_w, L0_ffn_w1, L0_ffn_b1, L0_ffn_w2, L0_ffn_b2), axis=-1)
    return x

_drawn_inputs = setup_inputs


def setup_inputs(seed=0):
    import zlib

    import numpy as np

    out = dict(_drawn_inputs(seed))
    spreads = {'L0_attn_bq': (0.0, 0.8),
     'L0_attn_bk': (0.0, 2.0),
     'L0_attn_bv': (0.0, 0.1),
     'L0_attn_bc2q': (0.0, 2.0),
     'L0_attn_bo': (0.0, 0.1),
     'L0_attn_g1': (1.0, 0.2),
     'L0_attn_beta1': (0.0, 0.1),
     'L0_attn_g2': (1.0, 0.2),
     'L0_attn_beta2': (0.0, 0.1),
     'L0_attn_b1': (0.0, 0.8),
     'L0_attn_bm': (0.0, 0.908),
     'L0_attn_bqo': (0.0, 0.1),
     'L0_attn_b2': (0.0, 0.1),
     'L0_ffn_b1': (0.0, 0.1),
     'L0_ffn_b2': (0.0, 0.1)}
    factors = {'L0_attn_Wq': 8.0,
     'L0_attn_Wk': 8.0,
     'L0_attn_Wv': 3.099,
     'L0_attn_Wc2q': 62.584,
     'L0_attn_W1': 4.124,
     'L0_attn_Wm': 3.587}
    for name, (base, spread) in spreads.items():
        noise = np.random.default_rng([zlib.crc32(name.encode()), seed]).standard_normal(out[name].shape)
        drawn = base * np.exp(spread * noise) if base else spread * noise
        out[name] = jnp.asarray(drawn.astype(out[name].dtype))
    for name, factor in factors.items():
        out[name] = (out[name] * factor).astype(out[name].dtype)
    return out
```

```python
from contextlib import ExitStack

import concourse.bass as bass
from concourse import mybir

F32 = mybir.dt.float32
BF16 = mybir.dt.bfloat16
FP16 = mybir.dt.float16
I32 = mybir.dt.int32
ALU = mybir.AluOpType
ACT = mybir.ActivationFunctionType
AX_X = mybir.AxisListType.X
AX_XY = mybir.AxisListType.XY
RMAX = bass.bass_isa.ReduceOp.max

P = 128
PI = 3.141592653589793
LN_EPS = 1e-05
EPS_COS = 1e-08
MAGIC = 1.5 * 2.0 ** 23


def bass_sandwich(
    nc: bass.Bass,
    x_d: bass.AP, Wq: bass.AP, bq: bass.AP, Wk: bass.AP, bk: bass.AP, Wv: bass.AP, bv: bass.AP,
    Wc2q: bass.AP, bc2q: bass.AP, Wo: bass.AP, bo: bass.AP, g1: bass.AP, beta1: bass.AP,
    g2: bass.AP, beta2: bass.AP, W1: bass.AP, b1: bass.AP, Wm: bass.AP, bm: bass.AP,
    Wqo: bass.AP, bqo: bass.AP, W2: bass.AP, b2: bass.AP, gate_w: bass.AP,
    ew1: bass.AP, eb1: bass.AP, ew2: bass.AP, eb2: bass.AP,
    out: bass.AP,
):
    NB, S, C = x_d.shape
    H, _, HD = Wq.shape
    NQ = Wc2q.shape[2]
    FF = W1.shape[1]
    NE, _, EF = ew1.shape
    assert C == P and H * HD == P and S == 2 * P and FF == 4 * P and EF == 4 * P
    TPB = S // P
    NT = NB * TPB
    GT = 4
    NG = NT // GT
    HW = NQ + HD
    SIDE = H * HW
    PW = 2 * SIDE + H * HD
    FC = FF // P
    EC = EF // P
    HP = H // 2
    UW = 2 * TPB * S
    VW = HD + 1
    KC = 6 * HD
    QBLK = 4 * NQ
    TS = 256
    RS = TS // P
    NS = NT * P // TS + NE
    ROW = 2 * C + 2
    assert PW == 512 and UW == 1024 and QBLK == 32

    ctx = ExitStack()
    with ctx:
        def sb(name, shape, dt=F32):
            return ctx.enter_context(nc.sbuf_tensor(name, shape, dt))

        def sem(name):
            return ctx.enter_context(nc.semaphore(name))

        ps = ctx.enter_context(nc.psum_tensor("ps", [P, 8, 512], F32))
        slot = [ps[:, 2 * i:2 * i + 2, :].rearrange("p a n -> p (a n)") for i in range(3)]
        tbank = ps[:, 6, :]
        hbank = ps[:, 7, :]

        x_all = sb("x_all", [P, NT, C])
        arena = sb("arena", [P, 13 * 512])
        proj = sb("proj", [P, NT, PW])
        s_off = [0]

        def setup(*dims):
            n = 1
            for d in dims:
                n *= d
            v = arena[:, s_off[0]:s_off[0] + n]
            s_off[0] += n
            if len(dims) == 1:
                return v
            return v.rearrange("p (a n) -> p a n", a=dims[0])

        wraw, wT, bcol_bc, qb_bc = setup(3, P), setup(2, P), setup(2, P), setup(2, P)
        w1_sb, w1T, w2_sb, b1c_bc = setup(FF), setup(FC, P), setup(FC, C), setup(FC, P)
        wqo9 = setup(FF)[0:NQ + 1, :]
        rt = arena[:, 0:6 * NT * NE].rearrange("p (a t e) -> p a t e", a=6, t=NT)
        mv_all = sb("mv_all", [P, 2, NT])
        n2 = sb("n2", [P, NT, 2 * H])
        inv = sb("inv", [P, NT, 2 * H])
        big = sb("big", [P, 2, HP, UW])
        tok = sb("tok", [P, 2816])
        vbuf = sb("vbuf", [P, 2, TPB, H * VW + 16])
        hT = sb("hT", [P, 512])
        wcat = sb("wcat", [P, PW])
        bias_bc = sb("bias_bc", [P, PW])
        bdiag = sb("bdiag", [P, H * NQ])
        bcol = sb("bcol", [P, 2])
        bc2q_bc = sb("bc2q_bc", [P, H * NQ])
        ident = sb("ident", [P, P])
        ident_b = sb("ident_b", [P, P], BF16)
        ident_h = sb("ident_h", [P, P], FP16)
        wo_sb = sb("wo_sb", [P, C])
        vec_bc = sb("vec_bc", [P, 5, C])
        bo_bc, g1_bc, be1_bc, g2_bc, be2_bc = (vec_bc[:, i, :] for i in range(5))
        wm_sb = sb("wm_sb", [P, FC, NQ])
        b1c = sb("b1c", [P, FC])
        bm_row = sb("bm_row", [1, NQ])
        wqoT = sb("wqoT", [P, FC, NQ + 1])
        b2_row = sb("b2_row", [1, C])
        xs_d = nc.dram_tensor("sorted_rows", [NS * TS, ROW], F32).ap()
        e9 = sb("e9", [1, NQ + 1])
        one = sb("one", [1, P])
        wA = sb("wA", [P, NQ])
        bA_bc = sb("bA_bc", [P, NQ])
        wB = sb("wB", [NQ + 1, C])
        stats = sb("stats", [P, GT, 6])
        mv = sb("mv", [P, GT, 2])
        veps = sb("veps", [P, GT])
        rstd = sb("rstd", [P, GT])
        mhalf = sb("mhalf", [P, NT])
        halfpi = sb("halfpi", [P, 1])
        gb = sb("gb", [P, 10, GT, P])
        at4, xnb4, aT4, y4, x14, x1T4, o4, xr4, xrT4, yy4 = (gb[:, i, :, :] for i in range(10))
        qm = sb("qm", [P, 4, GT, NQ])
        qe = sb("qe", [P, GT, NQ + 1])
        qeT = sb("qeT", [NQ + 1, GT * P])
        ln = sb("ln", [P, 4, GT, 10])
        lg = sb("lg", [P, NT, NE])
        gw_sb = sb("gw_sb", [P, NE])
        tri = sb("tri", [P, P])
        ones = sb("ones", [P, P])
        pref = sb("pref", [P, NE])
        tile_no = sb("tile_no", [P, NS])
        tok_id = sb("tok_id", [P, NT])
        rs = sb("rs", [P, 8, NT])
        sl_i = sb("sl_i", [P, NT], I32)
        exp_i = sb("exp_i", [P, NS], I32)
        eb1_sb = sb("eb1_sb", [P, NE, EC])
        eb2_sb = sb("eb2_sb", [P, NE])
        mxs = sb("mxs", [P, TPB, H])
        mneg = sb("mneg", [P, TPB, H])
        mtok = sb("mtok", [P, TPB, H, 2], BF16)
        hsum = sb("hsum", [P, TPB, H])
        small = sb("small", [P, 8])
        flag = sb("flag", [P, 1], I32)

        bigf = big[:, :, :, :].rearrange("p a u w -> p (a u w)")
        FW = EF + EC * C + RS * ROW + RS * P * (1 + EC + 1) + RS * C * 2
        def fbuf(par, off, n):
            return bigf[:, par * FW + off:par * FW + off + n]
        offs = [0]
        def take(n):
            offs.append(offs[-1] + n)
            return [fbuf(par, offs[-2], n) for par in range(2)]
        fw1 = take(EF)
        fw2 = [v.rearrange("p (c n) -> p c n", c=EC) for v in take(EC * C)]
        frow = [v.rearrange("p (t n) -> p t n", t=RS) for v in take(RS * ROW)]
        fxT = take(TS)
        fg = [v.rearrange("p (c n) -> p c n", c=EC) for v in take(EC * TS)]
        fyT = take(TS)
        fwy = [v.rearrange("p (t n) -> p t n", t=RS) for v in take(RS * C)]
        fres = [v.rearrange("p (t n) -> p t n", t=RS) for v in take(RS * C)]
        assert offs[-1] == FW and 2 * FW <= 2 * HP * UW
        fbias = sb("fbias", [P, 2, EC + 1])
        fidx_f = sb("fidx_f", [P, 2, RS])
        fidx = sb("fidx", [P, 2, RS], I32)
        fst = sb("fst", [P, 2, RS, 10])

        ar_b = arena[:, :].bitcast(BF16)
        ar_h = arena[:, :].bitcast(FP16)
        W_C = H * S
        OPW = 3 * W_C + 2 * S
        cqT = [ar_b[:, i * OPW:i * OPW + W_C].rearrange("p (h s) -> p h s", h=H) for i in range(2)]
        ckT = [ar_b[:, i * OPW + W_C:i * OPW + 2 * W_C].rearrange("p (h s) -> p h s", h=H) for i in range(2)]
        ukT = [ar_h[:, i * OPW + 2 * W_C:i * OPW + 3 * W_C].rearrange("p (h s) -> p h s", h=H) for i in range(2)]
        uqT = [ar_h[:, i * OPW + 3 * W_C:(i + 1) * OPW].rearrange("p (g s) -> p g s", g=2) for i in range(2)]

        tk_b = tok[:, :].bitcast(BF16)
        tk_h = tok[:, :].bitcast(FP16)
        cq_tok = tk_b[:, 0:768].rearrange("p (t h a d) -> p t h a d", t=TPB, h=H, a=3)
        ck_tok = tk_b[:, 768:1536].rearrange("p (t h a d) -> p t h a d", t=TPB, h=H, a=3)
        uk_tok = tk_h[:, 1536:1536 + 2048].rearrange("p (t h n) -> p t h n", t=TPB, h=H)
        uq_tok = tk_h[:, 3584:3584 + 512].rearrange("p (t h n) -> p t h n", t=TPB, h=H)
        scr = tok[:, 2048:2048 + 256].rearrange("p (t h d) -> p t h d", t=TPB, h=H)
        scr_u = tok[:, 2304:2304 + 128].rearrange("p (t h d) -> p t h d", t=TPB, h=H)

        W = [big[:, i, :, :] for i in range(2)]

        def qk_view(t0, s, lo, hi):
            return proj[:, bass.ds(t0, TPB), s * SIDE:(s + 1) * SIDE].rearrange(
                "p t (h n) -> p t h n", h=H)[:, :, :, lo:hi]

        consts_ready = sem("consts_ready")
        zeros_ready = sem("zeros_ready")
        x_loaded = [sem(f"x_loaded{i}") for i in range(4)]
        stood = sem("stood")
        qkv_loaded = sem("qkv_loaded")
        bd_loaded = sem("bd_loaded")
        post_loaded = sem("post_loaded")
        set_pe = sem("set_pe")
        set_cp = sem("set_cp")
        wcat_ready = sem("wcat_ready")
        st_dve = sem("st_dve")
        st_var = sem("st_var")
        st_rstd = sem("st_rstd")
        xn_ready = sem("xn_ready")
        xnT_ps = sem("xnT_ps")
        xnT_ready = sem("xnT_ready")
        proj_ps = sem("proj_ps")
        proj_ready = sem("proj_ready")
        nrm_sq = sem("nrm_sq")
        nrm_red = sem("nrm_red")
        nrm = sem("nrm")
        nrm_root = sem("nrm_root")
        inv_ready = sem("inv_ready")
        flag_all = sem("flag_all")
        flag_ready = sem("flag_ready")

        unit_ready = sem("unit_ready")
        unit_free = sem("unit_free")
        sin_ready = sem("sin_ready")
        w_ready = sem("w_ready")
        m_part = sem("m_part")
        m_tok = sem("m_tok")
        m_ps = sem("m_ps")
        m_T = sem("m_T")
        z_ready = sem("z_ready")
        p_ready = sem("p_ready")
        prep = sem("prep")
        prep_c = sem("prep_c")
        t_ps = sem("t_ps")
        t_act = sem("t_act")
        t_dve = sem("t_dve")
        pv_done = sem("pv_done")
        h_sb = sem("h_sb")
        h_tr = sem("h_tr")
        h_rec = sem("h_rec")
        h_done = sem("h_done")
        zfill = sem("zfill")
        z_stored = sem("z_stored")
        step = {n: sem("c_" + n) for n in (
            "at at_ps aT wo_ps xnb y st_a var_a r_a x1 x1_ps x1T qm_ps v0 v1 v2 v3 ang tanh cos qe qe_ps qeT ff_ps "
            "y2 nrm_o st_b var_b r_b o st_c var_c r_c x2a x2 st_d var_d r_d xr xr_ps xrT lg_ps lg rows na nb "
            "ea eb ec ed").split()}
        rsem = {n: sem("r_" + n) for n in "d p e i s".split()}
        scat = sem("scat")
        f_w = [sem("f_w0"), sem("f_w1")]
        f_rows = [sem("f_rows0"), sem("f_rows1")]
        f_out = [sem("f_out0"), sem("f_out1")]
        fs = {n: sem("f_" + n) for n in (
            "bias xT_ps xT h_ps g y_ps yT y_tr wy st var r veps idx idxa nrm res stat").split()}
        g_src = sem("g_src")
        g_tr = sem("g_tr")
        g_rows = sem("g_rows")
        g_mask = sem("g_mask")
        g_ps = sem("g_ps")
        g_min = sem("g_min")
        g_f = sem("g_f")

        g_norm = gb[:, 2, 0, 0:TPB * 2 * H].rearrange("p (t h) -> p t h", t=TPB)
        g_row = gb[0:H, 3, :, :].rearrange("p t n -> p (t n)")
        g_qrow = gb[0:H, 4, :, :].rearrange("p t n -> p (t n)")
        g_cos = gb[:, 0:2, :, :].rearrange("p a t n -> p (a t n)")
        xstat = sb("xstat", [P, 2, GT])

        def c_loop(eng, body):
            body(0, True, False, True)
            with eng.Fori(1, NG - 1) as g:
                body(g, True, True, True)
            body(NG - 1, True, True, False)
            body(NG, False, True, False)

        def f_loop(eng, body):
            body(0, 0, True, False)
            body(1, 1, True, False)
            with eng.Fori(1, NS // 2 - 1) as i:
                s = eng.snap(2 * i)
                body(s, 0, False, False)
                s = eng.snap(2 * i + 1)
                body(s, 1, False, False)
            body(NS - 2, 0, False, False)
            body(NS - 1, 1, False, True)

        def apart(eng):
            eng.sem_inc(stood, 1)

        block = ctx.enter_context(nc.Block())

        def cq_block(tt, h, i):
            return cq_tok[:, tt, h, i // 2:i // 2 + 2, :].rearrange("p a d -> p (a d)")

        def ck_block(tt, h, i):
            j = 1 if i == 0 else 0
            return ck_tok[:, tt, h, j:j + 2, :].rearrange("p a d -> p (a d)")

        def uq_block(tt, g):
            return uq_tok[:, tt, 4 * g:4 * g + 4, :].rearrange("p h n -> p (h n)")

        tb = tbank.bitcast(BF16)
        th = tbank.bitcast(FP16)

        T_BY = ["act", "dve", "act", "dve", "act", "act", "dve"]

        def t_dst(par, n):
            if n < 2:
                return cqT[par][0:KC, 4 * n:4 * n + 4, :].rearrange("p h s -> p (h s)"), tb[0:KC, 0:4 * S]
            if n < 4:
                return ckT[par][0:KC, 4 * n - 8:4 * n - 4, :].rearrange("p h s -> p (h s)"), tb[0:KC, 0:4 * S]
            if n < 6:
                return ukT[par][:, 4 * n - 16:4 * n - 12, :].rearrange("p h s -> p (h s)"), th[:, 0:4 * S]
            return uqT[par][:, :, :].rearrange("p g s -> p (g s)"), th[:, 0:2 * S]

        def act_before(b, n):
            return b * T_BY.count("act") + T_BY[:n].count("act")

        def dve_before(b, n):
            return 1 + b * T_BY.count("dve") + T_BY[:n].count("dve")

        def batches(eng, body, slow):
            body(0, 0, True, False, slow)
            with eng.Fori(0, (NB - 2) // 2) as i:
                b = eng.snap(i * 2 + 1)
                body(b, 1, False, False, slow)
                b = eng.snap(i * 2 + 2)
                body(b, 0, False, False, slow)
            body(NB - 1, (NB - 1) % 2, False, True, slow)

        def either(eng, body):
            eng.wait_ge(flag_ready, 1)
            v = eng.value_load(flag[0:1, 0:1], min_val=0, max_val=1)
            with eng.If(v != 0):
                batches(eng, body, True)
            with eng.Else():
                batches(eng, body, False)

        @block.sync
        def _(sp):
            xv = x_d.rearrange("b (t p) c -> p (b t) c", p=P)
            n = NT // 4
            for i in range(4):
                sp.dma_start(x_all[:, i * n:(i + 1) * n, :], xv[:, i * n:(i + 1) * n, :]).then_inc(x_loaded[i], 16)
            sp.wait_ge(zeros_ready, 1)
            for h in range(H):
                sp.dma_start(bdiag[HD * h:HD * h + HD, NQ * h:NQ * h + NQ], Wc2q[h]).then_inc(bd_loaded, 16)
            sp.dma_start(w1_sb[:, :], W1).then_inc(post_loaded, 16)
            sp.dma_start(wm_sb[:, :, :], Wm.rearrange("(c p) n -> p c n", p=P)).then_inc(post_loaded, 16)
            sp.dma_start(b1c[:, :], b1.rearrange("(c p) -> p c", p=P), allow_slow_non_contiguous=True).then_inc(post_loaded, 16)
            sp.dma_start(bm_row[:, :], bm.rearrange("(a n) -> a n", a=1)).then_inc(post_loaded, 16)
            sp.dma_start(wqo9[0:NQ, :], Wqo).then_inc(post_loaded, 16)
            sp.dma_start(wqo9[NQ:NQ + 1, :], bqo.rearrange("(a n) -> a n", a=1)).then_inc(post_loaded, 16)
            sp.dma_start(w2_sb[:, :, :], W2.rearrange("(c p) n -> p c n", p=P)).then_inc(post_loaded, 16)
            sp.dma_start(b2_row[:, :], b2.rearrange("(a n) -> a n", a=1)).then_inc(post_loaded, 16)
            sp.dma_start(wo_sb[:, :], Wo).then_inc(post_loaded, 16)
            for i, v in enumerate((bo, g1, beta1, g2, beta2)):
                sp.dma_start(vec_bc[:, i, :], v.partition_broadcast(P)).then_inc(post_loaded, 16)
            sp.dma_start(gw_sb[:, :], gate_w).then_inc(post_loaded, 16)
            sp.dma_start(eb1_sb[:, :, :], eb1.rearrange("e (c p) -> p e c", p=P), allow_slow_non_contiguous=True).then_inc(post_loaded, 16)
            sp.dma_start(eb2_sb[:, :], eb2.rearrange("e p -> p e"), allow_slow_non_contiguous=True).then_inc(post_loaded, 16)
            sp.wait_ge(zfill, 1)
            zc = NS * TS * ROW // P // 4
            zv = xs_d.rearrange("(q p r) n -> q p (r n)", q=4, p=P)
            for i in range(4):
                sp.dma_start(zv[i], big[:, :, :, :].rearrange("p a u w -> p (a u w)")[:, 0:zc]).then_inc(z_stored, 16)
            sp.wait_ge(rsem["i"], 2)
            sp.wait_ge(scat, 16 * NT)

            def tile_in(s, par, first):
                e = sp.value_load(exp_i[0:1, s:s + 1] if isinstance(s, int) else exp_i[0:1, bass.ds(s, 1)],
                                  min_val=0, max_val=NE - 1)
                if not first:
                    sp.wait_ge(fs["y_ps"], s - 1)
                    sp.wait_ge(fs["res"], s - 1)
                sp.dma_start(fw1[par], ew1[bass.ds(e, 1)].rearrange("e c f -> (e c) f")).then_inc(f_w[par], 16)
                sp.dma_start(fw2[par], ew2[bass.ds(e, 1)].rearrange("e (c p) n -> p (e c) n", p=P)).then_inc(f_w[par], 16)
                sp.dma_start(frow[par], xs_d.rearrange("(s t p) n -> s p t n", p=P, t=RS)[bass.ds(s, 1)].rearrange(
                    "s p t n -> p (s t) n")).then_inc(f_rows[par], 16)
            tile_in(0, 0, True)
            tile_in(1, 1, True)
            with sp.Fori(1, NS // 2) as i:
                for par in range(2):
                    tile_in(sp.snap(2 * i + par), par, False)
            sp.wait_ge(f_out[0], 16 * RS * NS // 2)
            sp.wait_ge(f_out[1], 16 * RS * NS // 2)

        @block.gpsimd
        def _(pool):
            pool.sem_inc(step["rows"], 1)
            nc.gpsimd.memset(bdiag[:, :], 0.0).then_inc(zeros_ready, 1)
            nc.gpsimd.memset(ident[:, :], 0.0).then_inc(consts_ready, 1)
            nc.gpsimd.memset(ident_b[:, :], 0.0).then_inc(consts_ready, 1)
            nc.gpsimd.memset(ident_h[:, :], 0.0).then_inc(consts_ready, 1)
            pool.wait_ge(consts_ready, 3)
            for m in (ident, ident_b, ident_h):
                nc.gpsimd.affine_select(out=m[:, :], in_=m[:, :], compare_op=ALU.not_equal, fill=1.0, base=0,
                                        pattern=[[-1, P]], channel_multiplier=1).then_inc(consts_ready, 1)
            nc.gpsimd.memset(mhalf[:, :], -0.5).then_inc(consts_ready, 1)
            nc.gpsimd.memset(one[:, :], 1.0).then_inc(consts_ready, 1)
            nc.gpsimd.memset(tok[:, :], 0.0).then_inc(consts_ready, 1)
            nc.gpsimd.memset(vbuf[:, :, :, :], 1.0).then_inc(consts_ready, 1)
            nc.gpsimd.memset(halfpi[:, :], PI / 2).then_inc(consts_ready, 1)
            nc.gpsimd.memset(e9[:, :], 0.0).then_inc(consts_ready, 1)
            nc.gpsimd.memset(qe[:, :, :], 1.0).then_inc(consts_ready, 1)
            nc.gpsimd.memset(ones[:, :], 1.0).then_inc(consts_ready, 1)
            pool.wait_ge(consts_ready, 14)
            nc.gpsimd.memset(e9[:, NQ:NQ + 1], 1.0).then_inc(consts_ready, 1)
            nc.gpsimd.affine_select(out=tri[:, :], in_=ones[:, :], compare_op=ALU.is_gt, fill=0.0, base=0,
                                    pattern=[[1, P]], channel_multiplier=-1).then_inc(consts_ready, 1)
            nc.gpsimd.iota(pref[:, :], pattern=[[-1, NE]], base=NE, channel_multiplier=0,
                           allow_small_or_imprecise_dtypes=True).then_inc(consts_ready, 1)
            nc.gpsimd.iota(tile_no[:, :], pattern=[[1, NS]], base=0, channel_multiplier=0,
                           allow_small_or_imprecise_dtypes=True).then_inc(consts_ready, 1)
            nc.gpsimd.iota(tok_id[:, :], pattern=[[P, NT]], base=1, channel_multiplier=1,
                           allow_small_or_imprecise_dtypes=True).then_inc(consts_ready, 1)
            def pool_rstd(n):
                pool.wait_ge(st_var, n + 1)
                apart(pool)
                nc.gpsimd.tensor_scalar(veps[:, :], mv[:, :, 1], LN_EPS, None, ALU.add).then_inc(st_rstd, 1)
                pool.wait_ge(st_rstd, 2 * n + 1)
                nc.gpsimd.tensor_tensor(rstd[:, :], veps[:, :], mhalf[:, 0:GT], ALU.pow).then_inc(st_rstd, 1)

            def squares(g):
                pool.wait_ge(proj_ready, (g + 2) * GT)
                for i in range(GT):
                    q = proj[:, bass.ds(g * GT + i, 1), 0:2 * SIDE].rearrange("p t (h n) -> p (t h) n", h=2 * H)[:, :, 0:NQ]
                    if i == 0:
                        pool.wait_ge(nrm_red, g + 1)
                    sq = nc.gpsimd.tensor_tensor(gb[:, 2, i, :].rearrange("p (h n) -> p h n", h=2 * H), q, q, ALU.mult)
                sq.then_inc(nrm_sq, 1)

            pool_rstd(0)
            with pool.Fori(1, NG) as g:
                pool_rstd(g)
                squares(g - 1)
            squares(NG - 1)
            pool.wait_ge(flag_all, 2)
            nc.gpsimd.partition_all_reduce(small[:, 4:6], small[:, 2:4], P, RMAX).then_inc(flag_all, 1)

            def prep_batch(b, slow):
                t0 = b * TPB

                def chained(ins):
                    prep_count[0] += 1
                    ins.then_inc(prep_c, 1)
                    pool.wait_ge(prep_c, b * PREP_STEPS + prep_count[0])
                    apart(pool)

                prep_count = [0]
                for s, dst in ((0, cq_tok), (1, ck_tok)):
                    src = qk_view(t0, s, NQ, HW)
                    if not (isinstance(b, int) and b == 0):
                        pool.wait_ge(t_ps, (b - 1) * 7 + 2 + 2 * s)
                    a, c, e = (dst[:, :, :, o, :] for o in (1, 0, 2))
                    chained(nc.gpsimd.tensor_copy(a, src))
                    chained(nc.gpsimd.tensor_tensor(scr, src, a, ALU.subtract))
                    chained(nc.gpsimd.tensor_copy(c, scr))
                    nc.gpsimd.tensor_tensor(e, scr, c, ALU.subtract).then_inc(prep, 1)
                    pool.wait_ge(prep, b * 5 + 1 + s)
                for s in (1, 0):
                    src = qk_view(t0, s, 0, NQ)
                    if not (isinstance(b, int) and b == 0):
                        pool.wait_ge(t_ps, (b - 1) * 7 + (6 if s else 7))
                    by = inv[:, bass.ds(t0, TPB), s * H:(s + 1) * H].unsqueeze(3).to_broadcast([P, TPB, H, NQ])
                    chained(nc.gpsimd.tensor_tensor(scr_u, src, by, ALU.mult))
                    if s == 0:
                        parts = uq_tok.rearrange("p t h (r n) -> p (t h) r n", r=2)
                        ub = scr_u.rearrange("p t h n -> p (t h) n").unsqueeze(2).to_broadcast([P, TPB * H, 2, NQ])
                        chained(nc.gpsimd.tensor_copy(parts[:, :, :, 0:NQ], ub))
                        nc.gpsimd.tensor_tensor(parts[:, :, :, NQ:2 * NQ], ub, parts[:, :, :, 0:NQ],
                                                ALU.subtract).then_inc(prep, 1)
                    else:
                        for tt in range(TPB):
                            for g in range(2):
                                flat = uk_tok[:, tt, 4 * g:4 * g + 4, :].rearrange("p h n -> p (h n)")
                                hi = diag_view(flat, 0)
                                lo = diag_view(flat, 2 * NQ)
                                u = scr_u[:, tt, 4 * g:4 * g + 4, :]
                                ub = u.unsqueeze(2).to_broadcast([P, 4, 2, NQ])
                                chained(nc.gpsimd.tensor_copy(hi, ub))
                                last = nc.gpsimd.tensor_tensor(lo, ub, hi, ALU.subtract)
                                if tt == TPB - 1 and g == 1:
                                    last.then_inc(prep, 1)
                                    pool.wait_ge(prep, b * 5 + 3)
                                else:
                                    chained(last)
                return t0

            def diag_view(flat, off):
                v = flat[:, off:off + 1]
                ap = [list(d) for d in v.ap]
                return bass.AP(v.tensor, v.offset, [ap[0], [P + QBLK, 4], [NQ, 2], [1, NQ]])

            PREP_STEPS = 3 + 3 + 1 + 4 + 3 + 2

            def prep_v(b, par):
                if not (isinstance(b, int) and b < 2):
                    pool.wait_ge(pv_done, b)
                v = vbuf[:, par, :, 0:H * VW].rearrange("p t (h n) -> p t h n", h=H)[:, :, :, 0:HD]
                src = proj[:, bass.ds(b * TPB, TPB), 2 * SIDE:PW].rearrange("p t (h n) -> p t h n", h=H)
                nc.gpsimd.tensor_copy(v, src).then_inc(prep, 1)

            pool.wait_ge(inv_ready, 1)
            def body(b, par, first, last, slow):
                prep_batch(b, slow)
                prep_v(b, par)
            batches(pool, body, False)

            pool.wait_ge(h_done, NB + 1)

            def rstd_c(k, name, n):
                pool.wait_ge(step["var_" + name], n + 1)
                apart(pool)
                nc.gpsimd.tensor_scalar(ln[:, k, :, 8], ln[:, k, :, 7], LN_EPS, None, ALU.add).then_inc(step["e" + name], 1)
                pool.wait_ge(step["e" + name], n + 1)
                nc.gpsimd.tensor_tensor(ln[:, k, :, 9], ln[:, k, :, 8], mhalf[:, 0:GT], ALU.pow).then_inc(step["r_" + name], 1)

            def xnb(g):
                if not (isinstance(g, int) and g == 0):
                    pool.wait_ge(step["y"], g)
                nc.gpsimd.tensor_copy(xnb4, x_all[:, bass.ds(g * GT, GT), :]).then_inc(step["nb"], 1)
                pool.wait_ge(step["nb"], 2 * g + 1)
                apart(pool)
                for i in range(GT):
                    ts = nc.gpsimd.tensor_scalar(xnb4[:, i, :], xnb4[:, i, :], xstat[:, 0, i:i + 1], xstat[:, 1, i:i + 1],
                                                 ALU.subtract, ALU.mult)
                ts.then_inc(step["nb"], 1)
                pool.wait_ge(step["nb"], 2 * g + 2)
                nc.gpsimd.tensor_tensor(xnb4, xnb4, bo_bc.unsqueeze(1).to_broadcast([P, GT, C]), ALU.add).then_inc(step["xnb"], 1)

            def xstats(g):
                nc.gpsimd.tensor_copy(xstat[:, :, :], mv_all[:, :, bass.ds(g * GT, GT)]).then_inc(step["na"], 1)
                pool.wait_ge(step["na"], g + 1)

            def c_body(g, one_, two, more):
                if one_:
                    rstd_c(0, "a", g)
                if two:
                    rstd_c(1, "b", g - 1)
                if more:
                    xstats(g + 1)
                    xnb(g + 1)
                if two:
                    rstd_c(2, "c", g - 1)
                    rstd_c(3, "d", g - 1)
                    pool.wait_ge(step["xr"], g)
                    nc.gpsimd.tensor_copy(proj[:, bass.ds((g - 1) * GT, GT), 0:C], xr4)
                    nc.gpsimd.tensor_copy(proj[:, bass.ds((g - 1) * GT, GT), 2 * C + 1], tok_id[:, bass.ds((g - 1) * GT, GT)]).then_inc(step["rows"], 1)

            xstats(0)
            xnb(0)
            c_loop(pool, c_body)

            pool.wait_ge(rsem["i"], 2)
            pool.wait_ge(step["rows"], NG + 1)
            pool.wait_ge(z_stored, 64)
            for t in range(NT):
                nc.gpsimd.indirect_dma_start(xs_d, bass.IndirectOffsetOnAxis(ap=sl_i[:, t:t + 1], axis=0),
                                             proj[:, t, 0:ROW], None).then_inc(scat, 16)

            out2 = out.rearrange("b s c -> (b s) c")

            def f_bias(s, par):
                e = pool.value_load(exp_i[0:1, s:s + 1] if isinstance(s, int) else exp_i[0:1, bass.ds(s, 1)],
                                    min_val=0, max_val=NE - 1)
                if not (isinstance(s, int) and s < 2):
                    pool.wait_ge(fs["yT"], s - 1)
                nc.gpsimd.tensor_copy(fbias[:, par, 0:EC], eb1_sb[:, bass.ds(e, 1), :].rearrange("p e c -> p (e c)"))
                nc.gpsimd.tensor_copy(fbias[:, par, EC:EC + 1], eb2_sb[:, bass.ds(e, 1)]).then_inc(fs["bias"], 1)

            def f_tail(s, par, first):
                pool.wait_ge(fs["var"], s + 1)
                apart(pool)
                nc.gpsimd.tensor_scalar(fst[:, par, :, 8], fst[:, par, :, 7], LN_EPS, None, ALU.add).then_inc(fs["veps"], 1)
                pool.wait_ge(fs["veps"], s + 1)
                nc.gpsimd.tensor_tensor(fst[:, par, :, 9], fst[:, par, :, 8], mhalf[:, 0:RS], ALU.pow).then_inc(fs["r"], 1)
                pool.wait_ge(fs["idx"], s + 1)
                pool.wait_ge(fs["res"], s + 1)
                apart(pool)
                for j in range(RS):
                    nc.gpsimd.indirect_dma_start(out2, bass.IndirectOffsetOnAxis(ap=fidx[:, par, j:j + 1], axis=0),
                                                 fres[par][:, j, :], None, bounds_check=NT * P - 1,
                                                 oob_is_err=False).then_inc(f_out[par], 16)

            f_bias(0, 0)
            f_loop(pool, lambda s, par, first, last: (None if last else f_bias(s + 1, 1 - par), f_tail(s, par, first)))

        @block.scalar
        def _(act):
            act.sem_inc(xnT_ready, 1)
            for i, w in enumerate((Wq, Wk, Wv)):
                act.dma_start(wraw[:, i, :].rearrange("p (h d) -> p h d", h=H), w.rearrange("h c d -> c h d")).then_inc(qkv_loaded, 16)
            for i, v in enumerate((bq, bk)):
                act.dma_start(bcol[:, i:i + 1], v.rearrange("h (d a) -> (h d) a", a=1)).then_inc(qkv_loaded, 16)
                act.dma_start(qb_bc[:, i, :], v.rearrange("h d -> (h d)").partition_broadcast(P)).then_inc(qkv_loaded, 16)
            act.dma_start(bias_bc[:, 2 * SIDE:PW], bv.rearrange("h d -> (h d)").partition_broadcast(P)).then_inc(qkv_loaded, 16)
            act.dma_start(bc2q_bc[:, :], bc2q.rearrange("h n -> (h n)").partition_broadcast(P)).then_inc(qkv_loaded, 16)
            act.wait_ge(set_pe, 1)
            nc.scalar.copy(wT[:, :, :].rearrange("p a n -> p (a n)"), ps[:, 4, 0:2 * P]).then_inc(set_cp, 1)
            with act.Fori(0, NG) as g:
                act.wait_ge(xnT_ps, g + 1)
                act.wait_ge(proj_ps, g * GT + 1)
                nc.scalar.copy(gb[:, 1, :, :].rearrange("p t n -> p (t n)"), tbank).then_inc(xnT_ready, 1)
            act.wait_ge(nrm, 1)
            n2f = n2[:, :, :].rearrange("p t h -> p (t h)")
            nc.scalar.activation(inv[:, :, :].rearrange("p t h -> p (t h)"), n2f, ACT.Sqrt).then_inc(nrm_root, 1)

            def body(b, par, first, last, slow):
                def sin(n):
                    if slow:
                        act.wait_ge(g_f, b * HP + n + 1)
                        src = g_cos
                    else:
                        act.wait_ge(unit_ready, 12 * b + 2 * n + 2)
                        src = slot[(2 * n + 1) % 3]
                    if n == 0 and not (isinstance(b, int) and b < 2):
                        act.wait_ge(pv_done, b)
                    nc.scalar.activation(W[par][:, n, :], src, ACT.Sin, scale=PI * (1 - 1e-6)).then_inc(sin_ready, 1)

                def evac(n, b1, par1):
                    act.wait_ge(t_ps, 7 * b1 + n + 1)
                    dst, src = t_dst(par1, n)
                    nc.scalar.copy(dst, src).then_inc(t_act, 1)

                def nxt(n):
                    if not last:
                        evac(n, b + 1, 1 - par)

                if first:
                    for n in range(7):
                        if T_BY[n] == "act":
                            evac(n, 0, 0)
                sin(0)
                nxt(0)
                sin(1)
                sin(2)
                nxt(2)
                if not first:
                    act.wait_ge(pv_done, b + 1)
                    act.wait_ge(h_tr, b)
                    nc.scalar.copy(hT[:, :], hbank).then_inc(h_sb, 1)
                sin(3)
                nxt(4)
                nxt(5)
                for n in range(HP):
                    act.wait_ge(z_ready, HP * b + n + 1)
                    nc.scalar.activation(W[par][:, n, :], W[par][:, n, :], ACT.Exp).then_inc(p_ready, 1)
                if last:
                    act.wait_ge(pv_done, b + 2)
                    act.wait_ge(h_tr, b + 1)
                    nc.scalar.copy(hT[:, :], hbank).then_inc(h_sb, 1)

            act.wait_ge(z_stored, 64)
            either(act, body)

            def flat(v):
                return v.rearrange("p t n -> p (t n)")

            def copy_at(g):
                if not (isinstance(g, int) and g == 0):
                    act.wait_ge(step["at_ps"], g)
                nc.scalar.copy(at4, proj[:, bass.ds(g * GT, GT), 0:C]).then_inc(step["at"], 1)

            def c_body(g, one_, two, more):
                if one_:
                    act.wait_ge(step["at_ps"], g + 1)
                    nc.scalar.copy(flat(aT4), ps[:, 0, :]).then_inc(step["aT"], 1)
                    if more:
                        copy_at(g + 1)
                    act.wait_ge(step["x1_ps"], g + 1)
                    nc.scalar.copy(flat(x1T4), ps[:, 2, :]).then_inc(step["x1T"], 1)
                    act.wait_ge(step["v0"], g + 1)
                    nc.scalar.activation(qm[:, 2, :, :], qm[:, 0, :, :], ACT.Tanh).then_inc(step["tanh"], 1)
                    act.wait_ge(step["ang"], g + 1)
                    nc.scalar.activation(qm[:, 3, :, :], qm[:, 1, :, :], ACT.Sin, bias=halfpi[:, 0:1], scale=-2 * PI).then_inc(step["cos"], 1)
                if two:
                    act.wait_ge(step["xr_ps"], g)
                    nc.scalar.copy(flat(xrT4), ps[:, 6, :]).then_inc(step["xrT"], 1)
                if one_:
                    act.wait_ge(step["qe_ps"], g + 1)
                    nc.scalar.copy(qeT[:, :], ps[0:NQ + 1, 4, :]).then_inc(step["qeT"], 1)

            act.wait_ge(h_done, NB + 1)
            copy_at(0)
            c_loop(act, c_body)

            act.wait_ge(rsem["e"], 1)
            nc.scalar.activation(rt[:, 1, :, :], rt[:, 1, :, :], ACT.Exp).then_inc(rsem["s"], 1)

            def f_xT(s, par):
                act.wait_ge(fs["xT_ps"], s + 1)
                nc.scalar.copy(fxT[par], ps[:, 0, 0:TS]).then_inc(fs["xT"], 1)

            f_xT(0, 0)

            def f_body(s, par, first, last):
                if not last:
                    f_xT(s + 1, 1 - par)
                act.wait_ge(fs["bias"], s + 1)
                for c in range(EC):
                    act.wait_ge(fs["h_ps"], s * EC // 2 + c // 2 + 1 if isinstance(s, int) else s * (EC // 2) + c // 2 + 1)
                    nc.scalar.activation(fg[par][:, c, :], ps[:, 1 + 2 * par + c // 2, (c % 2) * TS:(c % 2 + 1) * TS], ACT.Gelu,
                                         bias=fbias[:, par, c:c + 1]).then_inc(fs["g"], 1)
                act.wait_ge(fs["y_ps"], s + 1)
                nc.scalar.activation(fyT[par], ps[:, 5 + 2 * par, 0:TS], ACT.Identity, bias=fbias[:, par, EC:EC + 1]).then_inc(fs["yT"], 1)

            f_loop(act, f_body)

        @block.tensor
        def _(pe):
            pe.sem_inc(proj_ps, 1)
            pe.sem_inc(pv_done, 1)
            pe.sem_inc(h_tr, 1)
            pe.wait_ge(consts_ready, 4)
            pe.wait_ge(qkv_loaded, 16 * 9)
            for i in range(2):
                mm = nc.tensor.transpose(ps[:, 4, i * P:(i + 1) * P], wraw[:, i, :], ident[:, :])
            mm.then_inc(set_pe, 1)
            pe.wait_ge(set_cp, 2)
            pe.wait_ge(bd_loaded, 16 * H)
            w = H * NQ
            for i in range(2):
                nc.tensor.matmul(ps[:, 5, i * w:(i + 1) * w], wT[:, i, :], bdiag[:, :], start=True, stop=True)
            for i in range(2):
                mm = nc.tensor.matmul(ps[:, 5, (2 + i) * w:(3 + i) * w], bcol_bc[:, i, :], bdiag[:, :], start=True, stop=True)
            mm.then_inc(set_pe, 1)
            with pe.Fori(0, NG) as g:
                pe.wait_ge(xn_ready, g + 1)
                pe.wait_ge(xnT_ready, g + 1)
                for i in range(GT):
                    mm = nc.tensor.transpose(tbank[:, i * P:(i + 1) * P], gb[:, 0, i, :], ident[:, :])
                mm.then_inc(xnT_ps, 1)
                pe.wait_ge(xnT_ready, g + 2)
                pe.wait_ge(wcat_ready, 1)
                for i in range(GT):
                    pe.wait_ge(proj_ready, g * GT + i + 1)
                    nc.tensor.matmul(ps[:, i, :], gb[:, 1, i, :], wcat[:, :], start=True, stop=True).then_inc(proj_ps, 1)
            pe.wait_ge(post_loaded, 16 * 17)
            pe.wait_ge(consts_ready, 16)
            pe.wait_ge(proj_ready, NT + GT)
            for i in range(FC):
                nc.tensor.transpose(ps[:, 0, i * P:(i + 1) * P], w1_sb[:, i * P:(i + 1) * P], ident[:, :])
            for i in range(FC):
                mm = nc.tensor.transpose(ps[:, 1, i * 16:i * 16 + NQ + 1], wqo9[:, i * P:(i + 1) * P],
                                         ident[0:NQ + 1, 0:NQ + 1])
            mm.then_inc(set_pe, 1)
            pe.wait_ge(set_cp, 4)
            for i in range(FC):
                nc.tensor.matmul(ps[:, 2, 0:NQ], w1T[:, i, :], wm_sb[:, i, :], start=(i == 0), stop=(i == FC - 1))
            for i in range(FC):
                nc.tensor.matmul(ps[:, 3, 0:NQ], b1c_bc[:, i, :], wm_sb[:, i, :], start=(i == 0), stop=False)
            nc.tensor.matmul(ps[:, 3, 0:NQ], one[:, :], bm_row[:, :], start=False, stop=True)
            for i in range(FC):
                nc.tensor.matmul(ps[0:NQ + 1, 4, 0:C], wqoT[:, i, :], w2_sb[:, i, :], start=(i == 0), stop=False)
            nc.tensor.matmul(ps[0:NQ + 1, 4, 0:C], e9[:, :], b2_row[:, :], start=False, stop=True).then_inc(set_pe, 1)
            pe.wait_ge(set_cp, 7)

            def body(b, par, first, last, slow):
                def scores(k):
                    if 3 <= k < 2 * HP + 3:
                        pe.wait_ge(unit_free, 2 * HP * b + k - 2)
                    elif k >= 2 * HP + 3:
                        pe.wait_ge(z_ready, HP * b + k - 2 * HP - 2)
                    elif not first:
                        pe.wait_ge(z_ready, HP * b + k - 2)
                    return slot[k % 3]

                def guard_unit(n):
                    pe.wait_ge(g_mask, HP * b + n + 1)
                    o = scores(2 * n + 2)
                    for h in range(2):
                        for kt in range(TPB):
                            c = (h * TPB + kt) * S
                            mm = nc.tensor.matmul(o[:, c:c + S], g_row[:, S + kt * P:S + (kt + 1) * P],
                                                  g_qrow[:, h * S:(h + 1) * S], start=True, stop=True)
                    mm.then_inc(g_ps, 1)
                    pe.wait_ge(g_min, HP * b + n + 1)

                def norm_rows():
                    pe.wait_ge(g_src, b + 1)
                    bank_free(b + 1, 0)
                    for s in range(2):
                        for tt in range(TPB):
                            c = s * S + tt * P
                            mm = nc.tensor.transpose(tbank[0:H, c:c + P], g_norm[:, tt, s * H:(s + 1) * H], ident[:, :])
                    mm.then_inc(g_tr, 1)
                    pe.wait_ge(g_rows, b + 1)

                def max_unit(n):
                    o = scores(2 * n)
                    for h in range(2):
                        for qt in range(TPB):
                            c = (h * TPB + qt) * S
                            mm = nc.tensor.matmul(o[:, c:c + S], cqT[par][0:KC, 2 * n + h, qt * P:(qt + 1) * P],
                                                  ckT[par][0:KC, 2 * n + h, :], start=True, stop=True)
                    mm.then_inc(unit_ready, 1)

                def cos_unit(n):
                    o = scores(2 * n + 1)
                    for h in range(2):
                        for kt in range(TPB):
                            c = (h * TPB + kt) * S
                            mm = nc.tensor.matmul(o[:, c:c + S], ukT[par][:, 2 * n + h, kt * P:(kt + 1) * P],
                                                  uqT[par][:, n // 2, :], start=True, stop=True)
                    mm.then_inc(unit_ready, 1)
                    if slow:
                        guard_unit(n)

                def logit_unit(n):
                    o = scores(2 * HP + n)
                    for h in range(2):
                        for kt in range(TPB):
                            c = (h * TPB + kt) * S
                            mm = nc.tensor.matmul(o[:, c:c + S], ckT[par][0:KC + 2, 2 * n + h, kt * P:(kt + 1) * P],
                                                  cqT[par][0:KC + 2, 2 * n + h, :], start=True, stop=True)
                    mm.then_inc(unit_ready, 1)

                def trans(n, b1):
                    pe.wait_ge(prep, b1 * 5 + [1, 1, 2, 2, 3, 3, 4][n])
                    bank_free(b1, n)
                    for tt in range(TPB):
                        if n < 4:
                            for h in range(4):
                                for i in range(3):
                                    blk = (cq_block if n < 2 else ck_block)(tt, 4 * (n % 2) + h, i)
                                    c = h * S + tt * P
                                    mm = nc.tensor.transpose(tb[32 * i:32 * i + 32, c:c + P], blk, ident_b[:, :])
                        elif n < 6:
                            for h in range(4):
                                c = h * S + tt * P
                                mm = nc.tensor.transpose(th[:, c:c + P], uk_tok[:, tt, 4 * (n - 4) + h, :], ident_h[:, :])
                        else:
                            for g in range(2):
                                c = g * S + tt * P
                                mm = nc.tensor.transpose(th[:, c:c + P], uq_block(tt, g), ident_h[:, :])
                    mm.then_inc(t_ps, 1)

                def bank_free(b1, n):
                    a, d = act_before(b1, n), dve_before(b1, n)
                    if not (isinstance(a, int) and a == 0):
                        pe.wait_ge(t_act, a)
                    if not (isinstance(d, int) and d == 0):
                        pe.wait_ge(t_dve, d)

                def nxt(n):
                    if not last:
                        trans(n, b + 1)

                def maxima(r):
                    pe.wait_ge(m_tok, b + 1)
                    if r == 0:
                        if last:
                            bank_free(b + 1, 0)
                        else:
                            bank_free(b + 1, 5)
                    else:
                        pe.wait_ge(m_T, 2 * b + 1)
                    for h in range(4):
                        for qt in range(TPB):
                            c = h * S + qt * P
                            mm = nc.tensor.transpose(tb[96:98, c:c + P], mtok[:, qt, 4 * r + h, :], ident_b[:, :])
                    mm.then_inc(m_ps, 1)

                def pv(b1, par1):
                    pe.wait_ge(p_ready, HP * (b1 + 1))
                    pe.wait_ge(prep, b1 * 5 + 5)
                    pe.wait_ge(h_done, b1 + 1)
                    for g in range(2):
                        for kt in range(TPB):
                            for j in range(4):
                                h = 4 * g + j
                                c = ((h % 2) * TPB + kt) * S
                                mm = nc.tensor.matmul(hbank[32 * j:32 * j + 32, g * S:(g + 1) * S],
                                                      vbuf[:, par1, kt, h * VW:h * VW + 32],
                                                      W[par1][:, h // 2, c:c + S], start=(kt == 0), stop=(kt == 1),
                                                      skip_group_check=True)
                    mm.then_inc(pv_done, 1)

                def heads_back(b1):
                    pe.wait_ge(h_sb, b1 + 1)
                    for tt in range(TPB):
                        for g in range(2):
                            c = (tt * 2 + g) * P
                            mm = nc.tensor.transpose(hbank[:, c:c + P], hT[:, g * S + tt * P:g * S + (tt + 1) * P], ident[:, :])
                    mm.then_inc(h_tr, 1)

                if first:
                    for n in range(7):
                        trans(n, 0)
                pe.wait_ge(t_act, act_before(b + 1, 0))
                pe.wait_ge(t_dve, dve_before(b + 1, 0))
                if slow:
                    norm_rows()
                max_unit(0)
                cos_unit(0)
                nxt(0)
                max_unit(1)
                cos_unit(1)
                if not first:
                    pv(b - 1, 1 - par)
                nxt(1)
                max_unit(2)
                cos_unit(2)
                nxt(2)
                max_unit(3)
                cos_unit(3)
                nxt(3)
                nxt(4)
                if not first:
                    heads_back(b - 1)
                maxima(0)
                maxima(1)
                pe.wait_ge(m_T, 2 * b + 2)
                logit_unit(0)
                nxt(5)
                logit_unit(1)
                nxt(6)
                logit_unit(2)
                logit_unit(3)
                if last:
                    pv(b, par)
                    heads_back(b)

            either(pe, body)

            def turned(bank, src, n=GT):
                for i in range(n):
                    mm = nc.tensor.transpose(bank[:, i * P:(i + 1) * P], src[:, i, :], ident[:, :])
                return mm

            def c_body(g, one_, two, more):
                if one_:
                    pe.wait_ge(step["at"], g + 1)
                    turned(ps[:, 0, :], at4).then_inc(step["at_ps"], 1)
                    pe.wait_ge(step["aT"], g + 1)
                    for i in range(GT):
                        mm = nc.tensor.matmul(ps[:, 1, i * P:(i + 1) * P], aT4[:, i, :], wo_sb[:, :], start=True, stop=True)
                    mm.then_inc(step["wo_ps"], 1)
                if two:
                    pe.wait_ge(step["qeT"], g)
                    for i in range(GT):
                        mm = nc.tensor.matmul(ps[:, 5, i * P:(i + 1) * P], qeT[:, i * P:(i + 1) * P], wB[:, :], start=True, stop=True)
                    mm.then_inc(step["ff_ps"], 1)
                if one_:
                    pe.wait_ge(step["x1"], g + 1)
                    turned(ps[:, 2, :], x14).then_inc(step["x1_ps"], 1)
                    pe.wait_ge(step["x1T"], g + 1)
                    for i in range(GT):
                        mm = nc.tensor.matmul(ps[:, 3, i * NQ:(i + 1) * NQ], x1T4[:, i, :], wA[:, :], start=True, stop=True)
                    mm.then_inc(step["qm_ps"], 1)
                if two:
                    pe.wait_ge(step["xr"], g)
                    turned(ps[:, 6, :], xr4).then_inc(step["xr_ps"], 1)
                if one_:
                    pe.wait_ge(step["qe"], g + 1)
                    for i in range(GT):
                        mm = nc.tensor.transpose(ps[0:NQ + 1, 4, i * P:(i + 1) * P], qe[:, i, :], ident[:, :])
                    mm.then_inc(step["qe_ps"], 1)
                if two:
                    pe.wait_ge(step["xrT"], g)
                    for i in range(GT):
                        mm = nc.tensor.matmul(ps[:, 7, i * NE:(i + 1) * NE], xrT4[:, i, :], gw_sb[:, :], start=True, stop=True)
                    mm.then_inc(step["lg_ps"], 1)

            pe.wait_ge(h_done, NB + 1)
            c_loop(pe, c_body)

            pe.wait_ge(rsem["p"], 1)
            m = rt[:, 0, :, :].rearrange("p t e -> p (t e)")
            nc.tensor.matmul(ps[:, 0, 0:NT * NE], tri[:, :], m, start=True, stop=True)
            nc.tensor.matmul(ps[:, 1, 0:NT * NE], ones[:, :], m, start=True, stop=True).then_inc(rsem["p"], 1)

            def f_in(s, par, first):
                pe.wait_ge(f_rows[par], 16 * (s // 2 + 1) if isinstance(s, int) else half(s))
                if not (isinstance(s, int) and s == 0):
                    pe.wait_ge(fs["xT"], s)
                for j in range(RS):
                    mm = nc.tensor.transpose(ps[:, 0, j * P:(j + 1) * P], frow[par][:, j, 0:C], ident[:, :])
                mm.then_inc(fs["xT_ps"], 1)

            def f_up(s, par, first):
                pe.wait_ge(f_w[par], 32 * (s // 2 + 1) if isinstance(s, int) else 2 * half(s))
                pe.wait_ge(fs["xT"], s + 1)
                for c in range(EC):
                    if c % 2 == 0 and not first:
                        pe.wait_ge(fs["g"], (s - 2) * EC + c + 2)
                    mm = nc.tensor.matmul(ps[:, 1 + 2 * par + c // 2, (c % 2) * TS:(c % 2 + 1) * TS],
                                          fw1[par][:, c * P:(c + 1) * P], fxT[par], start=True, stop=True)
                    if c % 2 == 1:
                        mm.then_inc(fs["h_ps"], 1)

            def f_down(s, par, first):
                if not first:
                    pe.wait_ge(fs["yT"], s - 1)
                for c in range(EC):
                    pe.wait_ge(fs["g"], s * EC + c + 1)
                    mm = nc.tensor.matmul(ps[:, 5 + 2 * par, 0:TS], fw2[par][:, c, :], fg[par][:, c, :], start=(c == 0), stop=(c == EC - 1))
                mm.then_inc(fs["y_ps"], 1)

            def f_back(s, par, first):
                pe.wait_ge(fs["yT"], s + 1)
                if not (isinstance(s, int) and s == 0):
                    pe.wait_ge(fs["wy"], s)
                for j in range(RS):
                    mm = nc.tensor.transpose(ps[:, 6, j * P:(j + 1) * P], fyT[par][:, j * P:(j + 1) * P], ident[:, :])
                mm.then_inc(fs["y_tr"], 1)

            def half(s):
                return (s - par_of[0]) * 8 + 16

            par_of = [0]
            pe.wait_ge(scat, 16 * NT)
            f_in(0, 0, True)
            f_up(0, 0, True)

            def f_body(s, par, first, last):
                par_of[0] = 1 - par
                if not last:
                    n_first = isinstance(s, int) and s == 0
                    f_in_n(s, par, n_first)
                f_down(s, par, first)
                f_back(s, par, first)

            def f_in_n(s, par, n_first):
                nxt_s = s + 1
                f_in(nxt_s, 1 - par, n_first)
                f_up(nxt_s, 1 - par, n_first)

            f_loop(pe, f_body)

        @block.vector
        def _(dve):
            dve.sem_inc(nrm_red, 1)
            dve.sem_inc(h_done, 1)
            nc.vector.memset(bigf[:, 0:NS * TS * ROW // P // 4], 0.0).then_inc(zfill, 1)
            dve.wait_ge(qkv_loaded, 16 * 9)
            for i in range(2):
                cp = nc.vector.tensor_copy(bcol_bc[:, i, :], bcol[:, i:i + 1].to_broadcast([P, P]))
            cp.then_inc(set_cp, 1)
            wq_v = wcat[:, 0:2 * SIDE].rearrange("p (a h n) -> p a h n", a=2, h=H)
            bq_v = bias_bc[:, 0:2 * SIDE].rearrange("p (a h n) -> p a h n", a=2, h=H)
            scale = [0.5 / HD ** 0.5, 1.0]
            for i in range(2):
                nc.vector.tensor_scalar(wq_v[:, i, :, NQ:HW], wraw[:, i, :].rearrange("p (h d) -> p h d", h=H),
                                        scale[i], None, ALU.mult)
                nc.vector.tensor_scalar(bq_v[:, i, :, NQ:HW], qb_bc[:, i, :].rearrange("p (h d) -> p h d", h=H),
                                        scale[i], None, ALU.mult)
            nc.vector.tensor_copy(wcat[:, 2 * SIDE:PW], wraw[:, 2, :])
            dve.wait_ge(set_pe, 2)
            w = H * NQ
            for i in range(2):
                nc.vector.tensor_copy(wq_v[:, i, :, 0:NQ], ps[:, 5, i * w:(i + 1) * w].rearrange("p (h n) -> p h n", h=H))
                last = nc.vector.tensor_tensor(bq_v[:, i, :, 0:NQ], ps[:, 5, (2 + i) * w:(3 + i) * w].rearrange("p (h n) -> p h n", h=H),
                                               bc2q_bc[:, :].rearrange("p (h n) -> p h n", h=H), ALU.add)
            last.then_inc(wcat_ready, 1)
            dve.sem_inc(proj_ready, GT)

            def ln_stats(src, n):
                for i in range(GT):
                    bs = nc.vector.bn_stats(stats[:, i, :], src(i))
                bs.then_inc(st_dve, 1)
                dve.wait_ge(st_dve, n + 1)
                apart(dve)
                for i in range(GT):
                    ag = nc.vector.bn_aggr(mv[:, i, :], stats[:, i, :])
                ag.then_inc(st_var, 1)

            def proj_out(g):
                for i in range(GT):
                    dve.wait_ge(proj_ps, g * GT + i + 2)
                    nc.vector.tensor_tensor(proj[:, bass.ds(g * GT + i, 1), :].rearrange("p t n -> p (t n)"), ps[:, i, :],
                                            bias_bc[:, :], ALU.add).then_inc(proj_ready, 1)

            def norm_out(g):
                dve.wait_ge(nrm_sq, g + 1)
                nc.vector.tensor_reduce(n2[:, bass.ds(g * GT, GT), :].rearrange("p t h -> p (t h)"),
                                        gb[:, 2, :, :].rearrange("p t (h n) -> p (t h) n", h=2 * H), AX_X, ALU.add).then_inc(nrm_red, 1)

            def x_norm(g):
                dve.wait_ge(st_rstd, 2 * g + 2)
                dve.wait_ge(xnT_ps, g)
                nc.vector.tensor_copy(mv_all[:, 0, bass.ds(g * GT, GT)], mv[:, :, 0])
                nc.vector.tensor_copy(mv_all[:, 1, bass.ds(g * GT, GT)], rstd[:, :])
                for i in range(GT):
                    xn = nc.vector.tensor_scalar(gb[:, 0, i, :], x_all[:, bass.ds(g * GT + i, 1), :].rearrange("p t c -> p (t c)"),
                                                 mv[:, i, 0:1], rstd[:, i:i + 1], ALU.subtract, ALU.mult)
                xn.then_inc(xn_ready, 1)

            def group_src(g):
                return lambda i: x_all[:, bass.ds(g * GT + i, 1), :].rearrange("p t c -> p (t c)")

            for i in range(4):
                dve.wait_ge(x_loaded[i], 16)
            ln_stats(group_src(0), 0)
            x_norm(0)
            with dve.Fori(1, NG) as g:
                dve.wait_ge(xn_ready, g)
                ln_stats(group_src(g), g)
                x_norm(g)
                proj_out(g - 1)
                norm_out(g - 1)
            proj_out(NG - 1)
            norm_out(NG - 1)
            dve.wait_ge(nrm_red, NG + 1)
            n2f = n2[:, :, :].rearrange("p t h -> p (t h)")
            for s in range(2):
                mn = nc.vector.tensor_reduce(small[:, s:s + 1], n2[:, :, s * H:(s + 1) * H], AX_XY, ALU.min)
            mn.then_inc(flag_all, 1)
            dve.wait_ge(flag_all, 1)
            nc.vector.tensor_scalar(small[:, 2:4], small[:, 0:2], -1.0, None, ALU.mult).then_inc(flag_all, 1)
            nc.vector.tensor_scalar(n2f, n2f, 2e-35, None, ALU.max).then_inc(nrm, 1)
            dve.wait_ge(post_loaded, 16 * 17)
            nc.vector.tensor_copy(b1c_bc[:, :, :], b1c[:, :].unsqueeze(2).to_broadcast([P, FC, P]))
            dve.wait_ge(set_pe, 3)
            nc.vector.tensor_copy(w1T[:, :, :].rearrange("p c n -> p (c n)"), ps[:, 0, :]).then_inc(set_cp, 1)
            nc.vector.tensor_copy(wqoT[:, :, :], ps[:, 1, 0:FC * 16].rearrange("p (c n) -> p c n", n=16)[:, :, 0:NQ + 1]).then_inc(set_cp, 1)
            dve.wait_ge(set_pe, 4)
            nc.vector.tensor_copy(wA[:, :], ps[:, 2, 0:NQ]).then_inc(set_cp, 1)
            nc.vector.tensor_copy(bA_bc[:, :], ps[:, 3, 0:NQ]).then_inc(set_cp, 1)
            nc.vector.tensor_copy(wB[:, :], ps[0:NQ + 1, 4, 0:C]).then_inc(set_cp, 1)
            invf = inv[:, :, :].rearrange("p t h -> p (t h)")
            y2 = gb[:, 3, :, :].rearrange("p t n -> p (t n)")
            dve.wait_ge(nrm_root, 1)
            nc.vector.reciprocal(invf, invf).then_inc(nrm, 1)
            dve.wait_ge(nrm, 2)
            nc.vector.tensor_tensor(y2, invf, invf, ALU.mult).then_inc(nrm, 1)
            dve.wait_ge(nrm, 3)
            nc.vector.tensor_tensor(y2, y2, n2f, ALU.mult).then_inc(nrm, 1)
            dve.wait_ge(nrm, 4)
            nc.vector.tensor_scalar(y2, y2, -0.5, 1.5, ALU.mult, ALU.add).then_inc(nrm, 1)
            dve.wait_ge(nrm, 5)
            nc.vector.tensor_tensor(invf, invf, y2, ALU.mult).then_inc(inv_ready, 1)
            dve.wait_ge(flag_all, 3)
            nc.vector.tensor_tensor(small[:, 6:7], small[:, 4:5], small[:, 5:6], ALU.mult).then_inc(flag_all, 1)
            dve.wait_ge(flag_all, 4)
            nc.vector.tensor_scalar(flag[:, :], small[:, 6:7], 1.001 * EPS_COS ** 2, None, ALU.is_lt).then_inc(flag_ready, 1)
            for i in range(2):
                cp = nc.vector.memset(ckT[i][96:98, :, :], 1.0)
            cp.then_inc(t_dve, 1)

            def body(b, par, first, last, slow):
                def top(n):
                    if slow:
                        if n == 0:
                            norms()
                        mask(n)
                    dve.wait_ge(unit_ready, 12 * b + 2 * n + 1)
                    src = slot[(2 * n) % 3].rearrange("p (h t k) -> p t h k", h=2, t=TPB)
                    nc.vector.tensor_reduce(mxs[:, :, 2 * n:2 * n + 2], src, AX_X, ALU.max).then_inc(unit_free, 1)

                def weight(n):
                    f = slot[(2 * n + 1) % 3]
                    if slow:
                        guard(n)
                    dve.wait_ge(sin_ready, HP * b + n + 1)
                    if slow:
                        f = g_cos
                    nc.vector.scalar_tensor_tensor(W[par][:, n, :], W[par][:, n, :], 10.0, f, ALU.add, ALU.mult).then_inc(unit_free, 1)

                def norms():
                    t0 = b * TPB
                    nc.vector.scalar_tensor_tensor(g_norm, n2[:, bass.ds(t0, TPB), :], EPS_COS ** -0.5, inv[:, bass.ds(t0, TPB), :],
                                                   ALU.mult, ALU.mult).then_inc(g_src, 1)
                    dve.wait_ge(g_tr, b + 1)
                    nc.vector.tensor_copy(g_row, tbank[0:H, :]).then_inc(g_rows, 1)
                    dve.wait_ge(g_rows, b + 1)

                def mask(n):
                    for h in range(2):
                        mk = nc.vector.tensor_scalar(g_qrow[:, h * S:(h + 1) * S], g_row[:, 0:S],
                                                     ident[0:H, 2 * n + h:2 * n + h + 1], None, ALU.mult)
                    mk.then_inc(g_mask, 1)

                def guard(n):
                    dve.wait_ge(g_ps, HP * b + n + 1)
                    nc.vector.tensor_scalar(g_cos, slot[(2 * n + 2) % 3], 1.0, None, ALU.min).then_inc(g_min, 1)
                    dve.wait_ge(g_min, HP * b + n + 1)
                    nc.vector.tensor_tensor(g_cos, g_cos, slot[(2 * n + 1) % 3], ALU.mult).then_inc(g_f, 1)
                    dve.wait_ge(g_f, HP * b + n + 1)

                def logits(n):
                    k = 2 * HP + n
                    dve.wait_ge(unit_ready, 12 * b + k + 1)
                    nc.vector.scalar_tensor_tensor(W[par][:, n, :], W[par][:, n, :], 0.05, slot[k % 3],
                                                   ALU.mult, ALU.add).then_inc(z_ready, 1)

                def evac(n, b1, par1):
                    dve.wait_ge(t_ps, 7 * b1 + n + 1)
                    dst, src = t_dst(par1, n)
                    nc.vector.tensor_copy(dst, src).then_inc(t_dve, 1)

                def nxt(n):
                    if not last:
                        evac(n, b + 1, 1 - par)

                def maxima():
                    dve.wait_ge(unit_free, 2 * HP * (b + 1))
                    nc.vector.tensor_scalar(mtok[:, :, :, 0], mxs[:, :, :], -1.0, None, ALU.mult).then_inc(m_part, 1)
                    dve.wait_ge(m_part, b + 1)
                    nc.vector.scalar_tensor_tensor(mtok[:, :, :, 1], mxs[:, :, :], -1.0, mtok[:, :, :, 0],
                                                   ALU.mult, ALU.subtract).then_inc(m_tok, 1)

                def maxima_out(r):
                    dve.wait_ge(m_ps, 2 * b + r + 1)
                    nc.vector.tensor_copy(cqT[par][96:98, 4 * r:4 * r + 4, :].rearrange("p h s -> p (h s)"),
                                          tb[96:98, 0:4 * S]).then_inc(m_T, 1)

                def heads(b1):
                    v = hbank.rearrange("p (t h n) -> p t h n", t=TPB, h=H)
                    dve.wait_ge(h_tr, b1 + 2)
                    nc.vector.reciprocal(hsum[:, :, :], v[:, :, :, HD]).then_inc(h_rec, 1)
                    dve.wait_ge(h_rec, b1 + 1)
                    o = proj[:, bass.ds(b1 * TPB, TPB), 0:C].rearrange("p t (h d) -> p t h d", h=H)
                    nc.vector.tensor_tensor(o, v[:, :, :, 0:HD], hsum[:, :, :].unsqueeze(3).to_broadcast([P, TPB, H, HD]),
                                            ALU.mult).then_inc(h_done, 1)

                if first:
                    for n in range(7):
                        if T_BY[n] == "dve":
                            evac(n, 0, 0)
                top(0)
                weight(0)
                top(1)
                weight(1)
                nxt(1)
                top(2)
                weight(2)
                top(3)
                weight(3)
                maxima()
                nxt(3)
                maxima_out(0)
                maxima_out(1)
                if not first:
                    heads(b - 1)
                logits(0)
                logits(1)
                nxt(6)
                logits(2)
                logits(3)
                if last:
                    heads(b)

            either(dve, body)

            dve.wait_ge(h_done, NB + 1)

            def stats_c(k, name, src, n):
                for i in range(GT):
                    bs = nc.vector.bn_stats(ln[:, k, i, 0:6], src(i))
                bs.then_inc(step["st_" + name], 1)
                dve.wait_ge(step["st_" + name], n + 1)
                apart(dve)
                for i in range(GT):
                    ag = nc.vector.bn_aggr(ln[:, k, i, 6:8], ln[:, k, i, 0:6])
                ag.then_inc(step["var_" + name], 1)

            def affine(k, src, dst, gain, shift, own, n):
                for i in range(GT):
                    s1 = nc.vector.scalar_tensor_tensor(src[:, i, :], src[:, i, :], ln[:, k, i, 6:7], gain, ALU.subtract, ALU.mult)
                s1.then_inc(own, 1)
                dve.wait_ge(own, n + 1)
                for i in range(GT):
                    s2 = nc.vector.scalar_tensor_tensor(dst[:, i, :], src[:, i, :], ln[:, k, i, 9:10], shift, ALU.mult, ALU.add)
                return s2

            def c_body(g, one_, two, more):
                if one_:
                    dve.wait_ge(step["wo_ps"], g + 1)
                    dve.wait_ge(step["xnb"], g + 1)
                    nc.vector.tensor_tensor(y4, ps[:, 1, :].rearrange("p (t n) -> p t n", t=GT), xnb4, ALU.add).then_inc(step["y"], 1)
                    dve.wait_ge(step["y"], g + 1)
                    stats_c(0, "a", lambda i: y4[:, i, :], g)
                if two:
                    dve.wait_ge(step["ff_ps"], g)
                    nc.vector.tensor_tensor(yy4, ps[:, 5, :].rearrange("p (t n) -> p t n", t=GT), x14, ALU.add).then_inc(step["y2"], 1)
                    dve.wait_ge(step["y2"], g)
                    stats_c(1, "b", lambda i: yy4[:, i, :], g - 1)
                if one_:
                    dve.wait_ge(step["r_a"], g + 1)
                    affine(0, y4, x14, g1_bc, be1_bc, step["v3"], g).then_inc(step["x1"], 1)
                if two:
                    dve.wait_ge(step["r_b"], g)
                    affine(1, yy4, o4, g2_bc, be2_bc, step["x2a"], g - 1).then_inc(step["o"], 1)
                    dve.wait_ge(step["o"], g)
                    stats_c(2, "c", lambda i: o4[:, i, :], g - 1)
                if one_:
                    dve.wait_ge(step["qm_ps"], g + 1)
                    nc.vector.tensor_tensor(qm[:, 0, :, :], ps[:, 3, 0:GT * NQ].rearrange("p (t n) -> p t n", t=GT),
                                            bA_bc[:, :].unsqueeze(1).to_broadcast([P, GT, NQ]), ALU.add).then_inc(step["v0"], 1)
                    dve.wait_ge(step["v0"], g + 1)
                    nc.vector.tensor_scalar(qm[:, 1, :, :], qm[:, 0, :, :], 0.125, MAGIC, ALU.mult, ALU.add).then_inc(step["v1"], 1)
                    dve.wait_ge(step["v1"], 2 * g + 1)
                    nc.vector.tensor_scalar(qm[:, 1, :, :], qm[:, 1, :, :], -MAGIC, None, ALU.add).then_inc(step["v1"], 1)
                    dve.wait_ge(step["v1"], 2 * g + 2)
                    nc.vector.scalar_tensor_tensor(qm[:, 1, :, :], qm[:, 0, :, :], 0.125, qm[:, 1, :, :], ALU.mult, ALU.subtract).then_inc(step["v2"], 1)
                    dve.wait_ge(step["v2"], 3 * g + 1)
                    nc.vector.scalar_tensor_tensor(qm[:, 1, :, :], qm[:, 1, :, :], -1.0, qm[:, 1, :, :], ALU.mult, ALU.max).then_inc(step["v2"], 1)
                    dve.wait_ge(step["v2"], 3 * g + 2)
                    nc.vector.tensor_scalar(qm[:, 1, :, :], qm[:, 1, :, :], 0.5, None, ALU.min).then_inc(step["ang"], 1)
                    nc.vector.sem_inc(step["v2"], 1)
                if two:
                    dve.wait_ge(step["r_c"], g)
                    for i in range(GT):
                        s1 = nc.vector.tensor_scalar(o4[:, i, :], o4[:, i, :], ln[:, 2, i, 6:7], ln[:, 2, i, 9:10], ALU.subtract, ALU.mult)
                    s1.then_inc(step["nrm_o"], 1)
                    dve.wait_ge(step["nrm_o"], g)
                    t0 = (g - 1) * GT
                    nc.vector.tensor_tensor(proj[:, bass.ds(t0, GT), C:2 * C], o4, x_all[:, bass.ds(t0, GT), :], ALU.add).then_inc(step["x2"], 1)
                    dve.wait_ge(step["x2"], g)
                    apart(dve)
                    x2t = lambda i: proj[:, bass.ds(t0 + i, 1), C:2 * C].rearrange("p t c -> p (t c)")
                    stats_c(3, "d", x2t, g - 1)
                if one_:
                    dve.wait_ge(step["tanh"], g + 1)
                    dve.wait_ge(step["cos"], g + 1)
                    nc.vector.tensor_tensor(qe[:, :, 0:NQ], qm[:, 2, :, :], qm[:, 3, :, :], ALU.mult).then_inc(step["qe"], 1)
                if two:
                    dve.wait_ge(step["r_d"], g)
                    dve.wait_ge(step["rows"], g)
                    for i in range(GT):
                        s1 = nc.vector.tensor_scalar(xr4[:, i, :], x2t(i), ln[:, 3, i, 6:7], ln[:, 3, i, 9:10], ALU.subtract, ALU.mult)
                    s1.then_inc(step["xr"], 1)
                    dve.wait_ge(step["lg_ps"], g)
                    nc.vector.tensor_copy(lg[:, bass.ds(t0, GT), :], ps[:, 7, 0:GT * NE].rearrange("p (t e) -> p t e", t=GT)).then_inc(step["lg"], 1)

            c_loop(dve, c_body)

            steps = [0]

            def own(ins):
                steps[0] += 1
                ins.then_inc(rsem["d"], 1)
                dve.wait_ge(rsem["d"], steps[0])

            def over_e(v):
                return v.unsqueeze(2).to_broadcast([P, NT, NE])

            dve.wait_ge(step["lg"], NG)
            own(nc.vector.tensor_reduce(rs[:, 0, :], lg[:, :, :], AX_X, ALU.max))
            nc.vector.tensor_tensor(rt[:, 1, :, :], lg[:, :, :], over_e(rs[:, 0, :]), ALU.subtract).then_inc(rsem["e"], 1)
            own(nc.vector.tensor_tensor(rt[:, 2, :, :], lg[:, :, :], over_e(rs[:, 0, :]), ALU.is_equal))
            own(nc.vector.tensor_tensor(rt[:, 2, :, :], rt[:, 2, :, :], pref[:, :].unsqueeze(1).to_broadcast([P, NT, NE]), ALU.mult))
            own(nc.vector.tensor_reduce(rs[:, 1, :], rt[:, 2, :, :], AX_X, ALU.max))
            nc.vector.tensor_tensor(rt[:, 0, :, :], rt[:, 2, :, :], over_e(rs[:, 1, :]), ALU.is_equal).then_inc(rsem["p"], 1)
            dve.wait_ge(rsem["p"], 2)
            own(nc.vector.tensor_copy(rt[:, 3, :, :], ps[:, 1, 0:NT * NE].rearrange("p (t e) -> p t e", t=NT)))
            for e in range(NE):
                sc = nc.vector.tensor_tensor_scan(rt[:, 4, :, e], ones[:, 0:NT], rt[:, 3, :, e], 0.0, ALU.mult, ALU.add)
            own(sc)
            cnt, til, end, beg = (rs[:, 2 + i, 0:NE] for i in range(4))
            own(nc.vector.tensor_scalar(cnt, rt[:, 4, NT - 1, :], 1.0 / TS, (TS - 1) / (2.0 * TS), ALU.mult, ALU.add))
            own(nc.vector.tensor_scalar(til, cnt, MAGIC, None, ALU.add))
            own(nc.vector.tensor_scalar(til, til, -MAGIC, None, ALU.add))
            own(nc.vector.tensor_tensor_scan(end, ones[:, 0:NE], til, 0.0, ALU.mult, ALU.add))
            own(nc.vector.tensor_tensor(beg, end, til, ALU.subtract))
            own(nc.vector.tensor_tensor(rt[:, 4, :, :], rt[:, 4, :, :], rt[:, 3, :, :], ALU.subtract))
            own(nc.vector.tensor_tensor(rt[:, 4, :, :], rt[:, 4, :, :], ps[:, 0, 0:NT * NE].rearrange("p (t e) -> p t e", t=NT), ALU.add))
            own(nc.vector.scalar_tensor_tensor(rt[:, 4, :, :], beg.unsqueeze(1).to_broadcast([P, NT, NE]), float(TS), rt[:, 4, :, :],
                                               ALU.mult, ALU.add))
            own(nc.vector.tensor_tensor(rt[:, 4, :, :], rt[:, 4, :, :], rt[:, 0, :, :], ALU.mult))
            own(nc.vector.tensor_reduce(rs[:, 6, :], rt[:, 4, :, :], AX_X, ALU.add))
            te = rt[:, 5, 0:NS, :]
            own(nc.vector.tensor_tensor(te, tile_no[:, :].unsqueeze(2).to_broadcast([P, NS, NE]),
                                        end.unsqueeze(1).to_broadcast([P, NS, NE]), ALU.is_ge))
            own(nc.vector.tensor_reduce(rs[:, 7, 0:NS], te, AX_X, ALU.add))
            nc.vector.tensor_scalar(exp_i[:, :], rs[:, 7, 0:NS], NE - 1.0, None, ALU.min).then_inc(rsem["i"], 1)
            dve.wait_ge(rsem["s"], 1)
            own(nc.vector.tensor_reduce(rs[:, 0, :], rt[:, 1, :, :], AX_X, ALU.add))
            nc.vector.reciprocal(proj[:, :, 2 * C], rs[:, 0, :])
            nc.vector.tensor_copy(sl_i[:, :], rs[:, 6, :]).then_inc(rsem["i"], 1)

            def f_body(s, par, first, last):
                dve.wait_ge(fs["y_tr"], s + 1)
                for j in range(RS):
                    wy = nc.vector.tensor_scalar(fwy[par][:, j, :], ps[:, 6, j * P:(j + 1) * P], frow[par][:, j, 2 * C:2 * C + 1],
                                                 None, ALU.mult)
                wy.then_inc(fs["wy"], 1)
                if not first:
                    dve.wait_ge(f_out[par], (s - par) * (8 * RS))
                nc.vector.tensor_scalar(fidx_f[:, par, :], frow[par][:, :, 2 * C + 1], 0.0, 2.0 * NT * P, ALU.is_equal, ALU.mult).then_inc(fs["idxa"], 1)
                dve.wait_ge(fs["wy"], s + 1)
                for j in range(RS):
                    st = nc.vector.bn_stats(fst[:, par, j, 0:6], fwy[par][:, j, :])
                st.then_inc(fs["st"], 1)
                dve.wait_ge(fs["idxa"], s + 1)
                nc.vector.scalar_tensor_tensor(fidx[:, par, :], fidx_f[:, par, :], -1.0, frow[par][:, :, 2 * C + 1], ALU.add, ALU.add).then_inc(fs["idx"], 1)
                dve.wait_ge(fs["st"], s + 1)
                apart(dve)
                for j in range(RS):
                    ag = nc.vector.bn_aggr(fst[:, par, j, 6:8], fst[:, par, j, 0:6])
                ag.then_inc(fs["var"], 1)
                dve.wait_ge(fs["r"], s + 1)
                for j in range(RS):
                    nr = nc.vector.tensor_scalar(fwy[par][:, j, :], fwy[par][:, j, :], fst[:, par, j, 6:7], fst[:, par, j, 9:10],
                                                 ALU.subtract, ALU.mult)
                nr.then_inc(fs["nrm"], 1)
                dve.wait_ge(fs["nrm"], s + 1)
                nc.vector.tensor_tensor(fres[par][:, :, :], fwy[par][:, :, :], frow[par][:, :, C:2 * C], ALU.add).then_inc(fs["res"], 1)

            f_loop(dve, f_body)


_INS = ['L0_attn_x', 'L0_attn_Wq', 'L0_attn_bq', 'L0_attn_Wk', 'L0_attn_bk', 'L0_attn_Wv', 'L0_attn_bv',
        'L0_attn_Wc2q', 'L0_attn_bc2q', 'L0_attn_Wo', 'L0_attn_bo', 'L0_attn_g1', 'L0_attn_beta1',
        'L0_attn_g2', 'L0_attn_beta2', 'L0_attn_W1', 'L0_attn_b1', 'L0_attn_Wm', 'L0_attn_bm',
        'L0_attn_Wqo', 'L0_attn_bqo', 'L0_attn_W2', 'L0_attn_b2', 'L0_ffn_gate_w', 'L0_ffn_w1',
        'L0_ffn_b1', 'L0_ffn_w2', 'L0_ffn_b2']
_OUTS = [((16, 256, 128), 'float32')]


def kernel(**inputs):
    import numpy as _np
    import concourse.bacc as _bacc
    from concourse import mybir as _mybir
    from concourse.bass_utils import run_bass_kernel_spmd as _run

    nc = _bacc.Bacc("TRN2", target_bir_lowering=False, num_devices=1)
    arrays, args = {}, []
    for name in _INS:
        a = _np.ascontiguousarray(inputs[name])
        arrays[f"in_{name}_dram"] = a
        args.append(nc.dram_tensor(f"in_{name}_dram", a.shape, _mybir.dt.from_np(a.dtype), kind="ExternalInput").ap())
    for i, (shape, dtype) in enumerate(_OUTS):
        dt = _mybir.dt.from_np(_np.dtype(dtype))
        args.append(nc.dram_tensor(f"out_{i}_dram", shape, dt, kind="ExternalOutput").ap())
    bass_sandwich(nc, *args)
    r = _run(nc, [arrays], core_ids=[0])
    got = tuple(r.results[0][f"out_{i}_dram"] for i in range(len(_OUTS)))
    return got[0]
```

```python
from contextlib import ExitStack

import concourse.bass as bass
from concourse import mybir

F32 = mybir.dt.float32
BF16 = mybir.dt.bfloat16
FP16 = mybir.dt.float16
I32 = mybir.dt.int32
ALU = mybir.AluOpType
ACT = mybir.ActivationFunctionType
AX_X = mybir.AxisListType.X
AX_XY = mybir.AxisListType.XY
RMAX = bass.bass_isa.ReduceOp.max

P = 128
PI = 3.141592653589793
LN_EPS = 1e-05
EPS_COS = 1e-08
MAGIC = 1.5 * 2.0 ** 23


def bass_sandwich(
    nc: bass.Bass,
    x_d: bass.AP, Wq: bass.AP, bq: bass.AP, Wk: bass.AP, bk: bass.AP, Wv: bass.AP, bv: bass.AP,
    Wc2q: bass.AP, bc2q: bass.AP, Wo: bass.AP, bo: bass.AP, g1: bass.AP, beta1: bass.AP,
    g2: bass.AP, beta2: bass.AP, W1: bass.AP, b1: bass.AP, Wm: bass.AP, bm: bass.AP,
    Wqo: bass.AP, bqo: bass.AP, W2: bass.AP, b2: bass.AP, gate_w: bass.AP,
    ew1: bass.AP, eb1: bass.AP, ew2: bass.AP, eb2: bass.AP,
    out: bass.AP,
):
    NB, S, C = x_d.shape
    H, _, HD = Wq.shape
    NQ = Wc2q.shape[2]
    FF = W1.shape[1]
    NE, _, EF = ew1.shape
    assert C == P and H * HD == P and S == 2 * P and FF == 4 * P and EF == 4 * P
    TPB = S // P
    NT = NB * TPB
    GT = 4
    NG = NT // GT
    HW = NQ + HD
    SIDE = H * HW
    PW = 2 * SIDE + H * HD
    FC = FF // P
    EC = EF // P
    HP = H // 2
    UW = 2 * TPB * S
    VW = HD + 1
    KC = 6 * HD
    QBLK = 4 * NQ
    TS = 256
    RS = TS // P
    NS = NT * P // TS + NE
    ROW = 2 * C + 2
    assert PW == 512 and UW == 1024 and QBLK == 32

    ctx = ExitStack()
    with ctx:
        def sb(name, shape, dt=F32):
            return ctx.enter_context(nc.sbuf_tensor(name, shape, dt))

        def sem(name):
            return ctx.enter_context(nc.semaphore(name))

        ps = ctx.enter_context(nc.psum_tensor("ps", [P, 8, 512], F32))
        slot = [ps[:, 2 * i:2 * i + 2, :].rearrange("p a n -> p (a n)") for i in range(3)]
        tbank = ps[:, 6, :]
        hbank = ps[:, 7, :]

        x_all = sb("x_all", [P, NT, C])
        arena = sb("arena", [P, 13 * 512])
        proj = sb("proj", [P, NT, PW])
        s_off = [0]

        def setup(*dims):
            n = 1
            for d in dims:
                n *= d
            v = arena[:, s_off[0]:s_off[0] + n]
            s_off[0] += n
            if len(dims) == 1:
                return v
            return v.rearrange("p (a n) -> p a n", a=dims[0])

        wraw, wT, bcol_bc, qb_bc = setup(3, P), setup(2, P), setup(2, P), setup(2, P)
        w1_sb, w1T, w2_sb, b1c_bc = setup(FF), setup(FC, P), setup(FC, C), setup(FC, P)
        wqo9 = setup(FF)[0:NQ + 1, :]
        rt = arena[:, 0:6 * NT * NE].rearrange("p (a t e) -> p a t e", a=6, t=NT)
        mv_all = sb("mv_all", [P, 2, NT])
        n2 = sb("n2", [P, NT, 2 * H])
        inv = sb("inv", [P, NT, 2 * H])
        big = sb("big", [P, 2, HP, UW])
        tok = sb("tok", [P, 2816])
        vbuf = sb("vbuf", [P, 2, TPB, H * VW + 16])
        hT = sb("hT", [P, 512])
        wcat = sb("wcat", [P, PW])
        bias_bc = sb("bias_bc", [P, PW])
        bdiag = sb("bdiag", [P, H * NQ])
        bcol = sb("bcol", [P, 2])
        bc2q_bc = sb("bc2q_bc", [P, H * NQ])
        ident = sb("ident", [P, P])
        ident_b = sb("ident_b", [P, P], BF16)
        ident_h = sb("ident_h", [P, P], FP16)
        wo_sb = sb("wo_sb", [P, C])
        vec_bc = sb("vec_bc", [P, 5, C])
        bo_bc, g1_bc, be1_bc, g2_bc, be2_bc = (vec_bc[:, i, :] for i in range(5))
        wm_sb = sb("wm_sb", [P, FC, NQ])
        b1c = sb("b1c", [P, FC])
        bm_row = sb("bm_row", [1, NQ])
        wqoT = sb("wqoT", [P, FC, NQ + 1])
        b2_row = sb("b2_row", [1, C])
        xs_d = nc.dram_tensor("sorted_rows", [NS * TS, ROW], F32).ap()
        e9 = sb("e9", [1, NQ + 1])
        one = sb("one", [1, P])
        wA = sb("wA", [P, NQ])
        bA_bc = sb("bA_bc", [P, NQ])
        wB = sb("wB", [NQ + 1, C])
        stats = sb("stats", [P, GT, 6])
        mv = sb("mv", [P, GT, 2])
        mhalf = sb("mhalf", [P, NT])
        halfpi = sb("halfpi", [P, 1])
        gb = sb("gb", [P, 10, GT, P])
        at4, xnb4, aT4, y4, x14, x1T4, o4, xr4, xrT4, yy4 = (gb[:, i, :, :] for i in range(10))
        qm = sb("qm", [P, 4, GT, NQ])
        qe = sb("qe", [P, GT, NQ + 1])
        qeT = sb("qeT", [NQ + 1, GT * P])
        ln = sb("ln", [P, 4, GT, 10])
        lg = sb("lg", [P, NT, NE])
        gw_sb = sb("gw_sb", [P, NE])
        tri = sb("tri", [P, P])
        ones = sb("ones", [P, P])
        pref = sb("pref", [P, NE])
        tile_no = sb("tile_no", [P, NS])
        tok_id = sb("tok_id", [P, NT])
        rs = sb("rs", [P, 8, NT])
        sl_i = sb("sl_i", [P, NT], I32)
        exp_i = sb("exp_i", [P, NS], I32)
        eb1_sb = sb("eb1_sb", [P, NE, EC])
        eb2_sb = sb("eb2_sb", [P, NE])
        mxs = sb("mxs", [P, TPB, H])
        mneg = sb("mneg", [P, TPB, H])
        mtok = sb("mtok", [P, TPB, H, 2], BF16)
        hsum = sb("hsum", [P, TPB, H])
        small = sb("small", [P, 8])
        flag = sb("flag", [P, 1], I32)

        DEPTH = 6
        def cut_up(flat, off, n, shape, depth):
            bufs = [flat[:, off + i * n:off + (i + 1) * n] for i in range(depth)]
            return bufs if shape is None else [v.rearrange("p (a n) -> p a n", a=shape) for v in bufs]

        bigf = big[:, :, :, :].rearrange("p a u w -> p (a u w)")
        xf = x_all[:, :, :].rearrange("p t c -> p (t c)")
        fw1 = cut_up(bigf, 0, EF, None, DEPTH)
        fw2 = cut_up(bigf, DEPTH * EF, EC * C, EC, DEPTH)
        frow = cut_up(xf, 0, RS * ROW, RS, DEPTH)
        a0 = 6 * NT * NE
        fg = cut_up(arena, a0, EC * TS, EC, 2)
        fxT = cut_up(arena, a0 + 2 * EC * TS, TS, None, 2)
        fyT = cut_up(arena, a0 + 2 * (EC + 1) * TS, TS, None, 2)
        fwy = cut_up(arena, a0 + 2 * (EC + 2) * TS, RS * C, RS, 2)
        fres = cut_up(arena, a0 + 2 * (EC + 3) * TS, RS * C, RS, DEPTH)
        assert a0 + (2 * EC + 6 + DEPTH) * TS <= 13 * 512 and NS % DEPTH == 0
        fbias = sb("fbias", [P, NS, EC + 1])
        fpart = sb("fpart", [P, NS, EC + 1])
        fidx_f = sb("fidx_f", [P, DEPTH, RS])
        fidx = sb("fidx", [P, DEPTH, RS], I32)
        fst = sb("fst", [P, 2, RS, 10])

        ar_b = arena[:, :].bitcast(BF16)
        ar_h = arena[:, :].bitcast(FP16)
        W_C = H * S
        OPW = 3 * W_C + 2 * S
        cqT = [ar_b[:, i * OPW:i * OPW + W_C].rearrange("p (h s) -> p h s", h=H) for i in range(2)]
        ckT = [ar_b[:, i * OPW + W_C:i * OPW + 2 * W_C].rearrange("p (h s) -> p h s", h=H) for i in range(2)]
        ukT = [ar_h[:, i * OPW + 2 * W_C:i * OPW + 3 * W_C].rearrange("p (h s) -> p h s", h=H) for i in range(2)]
        uqT = [ar_h[:, i * OPW + 3 * W_C:(i + 1) * OPW].rearrange("p (g s) -> p g s", g=2) for i in range(2)]

        tk_b = tok[:, :].bitcast(BF16)
        tk_h = tok[:, :].bitcast(FP16)
        cq_tok = tk_b[:, 0:768].rearrange("p (t h a d) -> p t h a d", t=TPB, h=H, a=3)
        ck_tok = tk_b[:, 768:1536].rearrange("p (t h a d) -> p t h a d", t=TPB, h=H, a=3)
        uk_tok = tk_h[:, 1536:1536 + 2048].rearrange("p (t h n) -> p t h n", t=TPB, h=H)
        uq_tok = tk_h[:, 3584:3584 + 512].rearrange("p (t h n) -> p t h n", t=TPB, h=H)
        scr = tok[:, 2048:2048 + 256].rearrange("p (t h d) -> p t h d", t=TPB, h=H)
        scr_u = tok[:, 2304:2304 + 128].rearrange("p (t h d) -> p t h d", t=TPB, h=H)

        W = [big[:, i, :, :] for i in range(2)]

        def qk_view(t0, s, lo, hi):
            return proj[:, bass.ds(t0, TPB), s * SIDE:(s + 1) * SIDE].rearrange(
                "p t (h n) -> p t h n", h=H)[:, :, :, lo:hi]

        consts_ready = sem("consts_ready")
        zeros_ready = sem("zeros_ready")
        x_loaded = [sem(f"x_loaded{i}") for i in range(4)]
        stood = sem("stood")
        qkv_loaded = sem("qkv_loaded")
        bd_loaded = sem("bd_loaded")
        post_loaded = sem("post_loaded")
        set_pe = sem("set_pe")
        set_cp = sem("set_cp")
        wcat_ready = sem("wcat_ready")
        st_dve = sem("st_dve")
        st_var = sem("st_var")
        st_rstd = sem("st_rstd")
        xn_ready = sem("xn_ready")
        xnT_ps = sem("xnT_ps")
        xnT_ready = sem("xnT_ready")
        proj_ps = sem("proj_ps")
        proj_ready = sem("proj_ready")
        nrm_sq = sem("nrm_sq")
        nrm_red = sem("nrm_red")
        nrm = sem("nrm")
        nrm_root = sem("nrm_root")
        inv_ready = sem("inv_ready")
        flag_all = sem("flag_all")
        flag_ready = sem("flag_ready")

        unit_ready = sem("unit_ready")
        unit_free = sem("unit_free")
        sin_ready = sem("sin_ready")
        w_ready = sem("w_ready")
        m_part = sem("m_part")
        m_tok = sem("m_tok")
        m_ps = sem("m_ps")
        m_T = sem("m_T")
        z_ready = sem("z_ready")
        p_ready = sem("p_ready")
        prep = sem("prep")
        prep_c = sem("prep_c")
        t_ps = sem("t_ps")
        t_act = sem("t_act")
        t_dve = sem("t_dve")
        pv_done = sem("pv_done")
        h_sb = sem("h_sb")
        h_tr = sem("h_tr")
        h_rec = sem("h_rec")
        h_done = sem("h_done")
        zfill = sem("zfill")
        z_stored = sem("z_stored")
        step = {n: sem("c_" + n) for n in (
            "at at_ps aT wo_ps xnb y st_a var_a r_a x1 x1_ps x1T qm_ps v0 v1 v2 v3 ang tanh cos qe qe_ps qeT ff_ps "
            "y2 nrm_o st_b var_b r_b o st_c var_c r_c x2a x2 st_d var_d r_d xr xr_ps xrT lg_ps lg rows na nb "
            "ea eb ec ed").split()}
        rsem = {n: sem("r_" + n) for n in "d p e x i s".split()}
        scat = sem("scat")
        f_w = [sem(f"f_w{i}") for i in range(DEPTH)]
        f_rows = [sem(f"f_rows{i}") for i in range(DEPTH)]
        f_out = [sem(f"f_out{i}") for i in range(DEPTH)]
        fs = {n: sem("f_" + n) for n in (
            "bias xT_ps xT h_ps g y_ps yT y_tr wy st var r veps idx idxa nrm res stat").split()}
        g_src = sem("g_src")
        g_tr = sem("g_tr")
        g_rows = sem("g_rows")
        g_mask = sem("g_mask")
        g_ps = sem("g_ps")
        g_min = sem("g_min")
        g_f = sem("g_f")

        g_norm = gb[:, 2, 0, 0:TPB * 2 * H].rearrange("p (t h) -> p t h", t=TPB)
        g_row = gb[0:H, 3, :, :].rearrange("p t n -> p (t n)")
        g_qrow = gb[0:H, 4, :, :].rearrange("p t n -> p (t n)")
        g_cos = gb[:, 0:2, :, :].rearrange("p a t n -> p (a t n)")
        xstat = sb("xstat", [P, 2, GT])

        def c_loop(eng, body):
            body(0, True, False, True)
            with eng.Fori(1, NG - 1) as g:
                body(g, True, True, True)
            body(NG - 1, True, True, False)
            body(NG, False, True, False)

        def f_loop(eng, body):
            for j in range(DEPTH):
                body(0, j)
            with eng.Fori(1, NS // DEPTH - 1) as i:
                i = eng.snap(i)
                for j in range(DEPTH):
                    body(i, j)
            for j in range(DEPTH):
                body(NS // DEPTH - 1, j)

        def after(i, j, d):
            return i + (j + d) // DEPTH, (j + d) % DEPTH

        def exists(i, j):
            return not isinstance(i, int) or 0 <= DEPTH * i + j < NS

        def apart(eng):
            eng.sem_inc(stood, 1)

        block = ctx.enter_context(nc.Block())

        def cq_block(tt, h, i):
            return cq_tok[:, tt, h, i // 2:i // 2 + 2, :].rearrange("p a d -> p (a d)")

        def ck_block(tt, h, i):
            j = 1 if i == 0 else 0
            return ck_tok[:, tt, h, j:j + 2, :].rearrange("p a d -> p (a d)")

        def uq_block(tt, g):
            return uq_tok[:, tt, 4 * g:4 * g + 4, :].rearrange("p h n -> p (h n)")

        tb = tbank.bitcast(BF16)
        th = tbank.bitcast(FP16)

        T_BY = ["act", "dve", "act", "dve", "act", "act", "act"]

        def t_dst(par, n):
            if n < 2:
                return cqT[par][0:KC, 4 * n:4 * n + 4, :].rearrange("p h s -> p (h s)"), tb[0:KC, 0:4 * S]
            if n < 4:
                return ckT[par][0:KC, 4 * n - 8:4 * n - 4, :].rearrange("p h s -> p (h s)"), tb[0:KC, 0:4 * S]
            if n < 6:
                return ukT[par][:, 4 * n - 16:4 * n - 12, :].rearrange("p h s -> p (h s)"), th[:, 0:4 * S]
            return uqT[par][:, :, :].rearrange("p g s -> p (g s)"), th[:, 0:2 * S]

        def act_before(b, n):
            return b * T_BY.count("act") + T_BY[:n].count("act")

        def dve_before(b, n):
            return 1 + b * T_BY.count("dve") + T_BY[:n].count("dve")

        def batches(eng, body, slow):
            body(0, 0, True, False, slow)
            with eng.Fori(0, (NB - 2) // 2) as i:
                b = eng.snap(i * 2 + 1)
                body(b, 1, False, False, slow)
                b = eng.snap(i * 2 + 2)
                body(b, 0, False, False, slow)
            body(NB - 1, (NB - 1) % 2, False, True, slow)

        def either(eng, body):
            eng.wait_ge(flag_ready, 1)
            v = eng.value_load(flag[0:1, 0:1], min_val=0, max_val=1)
            with eng.If(v != 0):
                batches(eng, body, True)
            with eng.Else():
                batches(eng, body, False)

        @block.sync
        def _(sp):
            xv = x_d.rearrange("b (t p) c -> p (b t) c", p=P)
            n = NT // 4
            for i in range(4):
                sp.dma_start(x_all[:, i * n:(i + 1) * n, :], xv[:, i * n:(i + 1) * n, :]).then_inc(x_loaded[i], 16)
            sp.wait_ge(zeros_ready, 1)
            for h in range(H):
                sp.dma_start(bdiag[HD * h:HD * h + HD, NQ * h:NQ * h + NQ], Wc2q[h]).then_inc(bd_loaded, 16)
            sp.dma_start(w1_sb[:, :], W1).then_inc(post_loaded, 16)
            sp.dma_start(wm_sb[:, :, :], Wm.rearrange("(c p) n -> p c n", p=P)).then_inc(post_loaded, 16)
            sp.dma_start(b1c[:, :], b1.rearrange("(c p) -> p c", p=P), allow_slow_non_contiguous=True).then_inc(post_loaded, 16)
            sp.dma_start(bm_row[:, :], bm.rearrange("(a n) -> a n", a=1)).then_inc(post_loaded, 16)
            sp.dma_start(wqo9[0:NQ, :], Wqo).then_inc(post_loaded, 16)
            sp.dma_start(wqo9[NQ:NQ + 1, :], bqo.rearrange("(a n) -> a n", a=1)).then_inc(post_loaded, 16)
            sp.dma_start(w2_sb[:, :, :], W2.rearrange("(c p) n -> p c n", p=P)).then_inc(post_loaded, 16)
            sp.dma_start(b2_row[:, :], b2.rearrange("(a n) -> a n", a=1)).then_inc(post_loaded, 16)
            sp.dma_start(wo_sb[:, :], Wo).then_inc(post_loaded, 16)
            for i, v in enumerate((bo, g1, beta1, g2, beta2)):
                sp.dma_start(vec_bc[:, i, :], v.partition_broadcast(P)).then_inc(post_loaded, 16)
            sp.dma_start(gw_sb[:, :], gate_w).then_inc(post_loaded, 16)
            sp.dma_start(eb1_sb[:, :, :], eb1.rearrange("e (c p) -> p e c", p=P), allow_slow_non_contiguous=True).then_inc(post_loaded, 16)
            sp.dma_start(eb2_sb[:, :], eb2.rearrange("e p -> p e"), allow_slow_non_contiguous=True).then_inc(post_loaded, 16)
            sp.wait_ge(zfill, 1)
            zc = NS * TS * ROW // P // 4
            zv = xs_d.rearrange("(q p r) n -> q p (r n)", q=4, p=P)
            for i in range(4):
                sp.dma_start(zv[i], big[:, :, :, :].rearrange("p a u w -> p (a u w)")[:, 0:zc]).then_inc(z_stored, 16)
            sp.wait_ge(rsem["x"], 1)

            def tile_in(i, j):
                s = DEPTH * i + j
                e = sp.value_load(exp_i[0:1, s:s + 1] if isinstance(s, int) else exp_i[0:1, bass.ds(s, 1)],
                                  min_val=0, max_val=NE - 1)
                if exists(i - 1, j):
                    sp.wait_ge(fs["y_ps"], s - DEPTH + 1)
                sp.dma_start(fw1[j], ew1[bass.ds(e, 1)].rearrange("e c f -> (e c) f")).then_inc(f_w[j], 16)
                sp.dma_start(fw2[j], ew2[bass.ds(e, 1)].rearrange("e (c p) n -> p (e c) n", p=P)).then_inc(f_w[j], 16)
                if exists(i - 1, j):
                    sp.wait_ge(fs["res"], s - DEPTH + 1)
                elif j == 0:
                    sp.wait_ge(scat, 16 * NT)
                sp.dma_start(frow[j], xs_d.rearrange("(s t p) n -> s p t n", p=P, t=RS)[bass.ds(s, 1)].rearrange(
                    "s p t n -> p (s t) n")).then_inc(f_rows[j], 16)

            for j in range(DEPTH):
                tile_in(0, j)
            with sp.Fori(1, NS // DEPTH) as i:
                i = sp.snap(i)
                for j in range(DEPTH):
                    tile_in(i, j)
            for j in range(DEPTH):
                sp.wait_ge(f_out[j], 16 * RS * NS // DEPTH)

        @block.gpsimd
        def _(pool):
            pool.sem_inc(step["rows"], 1)
            nc.gpsimd.memset(bdiag[:, :], 0.0).then_inc(zeros_ready, 1)
            nc.gpsimd.memset(ident[:, :], 0.0).then_inc(consts_ready, 1)
            nc.gpsimd.memset(ident_b[:, :], 0.0).then_inc(consts_ready, 1)
            nc.gpsimd.memset(ident_h[:, :], 0.0).then_inc(consts_ready, 1)
            pool.wait_ge(consts_ready, 3)
            for m in (ident, ident_b, ident_h):
                nc.gpsimd.affine_select(out=m[:, :], in_=m[:, :], compare_op=ALU.not_equal, fill=1.0, base=0,
                                        pattern=[[-1, P]], channel_multiplier=1).then_inc(consts_ready, 1)
            nc.gpsimd.memset(mhalf[:, :], -0.5).then_inc(consts_ready, 1)
            nc.gpsimd.memset(one[:, :], 1.0).then_inc(consts_ready, 1)
            nc.gpsimd.memset(tok[:, :], 0.0).then_inc(consts_ready, 1)
            nc.gpsimd.memset(vbuf[:, :, :, :], 1.0).then_inc(consts_ready, 1)
            nc.gpsimd.memset(halfpi[:, :], PI / 2).then_inc(consts_ready, 1)
            nc.gpsimd.memset(e9[:, :], 0.0).then_inc(consts_ready, 1)
            nc.gpsimd.memset(qe[:, :, :], 1.0).then_inc(consts_ready, 1)
            nc.gpsimd.memset(ones[:, :], 1.0).then_inc(consts_ready, 1)
            pool.wait_ge(consts_ready, 14)
            nc.gpsimd.memset(e9[:, NQ:NQ + 1], 1.0).then_inc(consts_ready, 1)
            nc.gpsimd.affine_select(out=tri[:, :], in_=ones[:, :], compare_op=ALU.is_gt, fill=0.0, base=0,
                                    pattern=[[1, P]], channel_multiplier=-1).then_inc(consts_ready, 1)
            nc.gpsimd.iota(pref[:, :], pattern=[[-1, NE]], base=NE, channel_multiplier=0,
                           allow_small_or_imprecise_dtypes=True).then_inc(consts_ready, 1)
            nc.gpsimd.iota(tile_no[:, :], pattern=[[1, NS]], base=0, channel_multiplier=0,
                           allow_small_or_imprecise_dtypes=True).then_inc(consts_ready, 1)
            nc.gpsimd.iota(tok_id[:, :], pattern=[[P, NT]], base=1, channel_multiplier=1,
                           allow_small_or_imprecise_dtypes=True).then_inc(consts_ready, 1)
            def pool_rstd(g):
                pool.wait_ge(st_var, g + 1)
                apart(pool)
                of_g = mv_all[:, 1, bass.ds(g * GT, GT)]
                nc.gpsimd.tensor_tensor(of_g, of_g, mhalf[:, 0:GT], ALU.pow).then_inc(st_rstd, 1)

            def squares(g):
                pool.wait_ge(proj_ready, (g + 2) * GT)
                for i in range(GT):
                    q = proj[:, bass.ds(g * GT + i, 1), 0:2 * SIDE].rearrange("p t (h n) -> p (t h) n", h=2 * H)[:, :, 0:NQ]
                    if i == 0:
                        pool.wait_ge(nrm_red, g + 1)
                    sq = nc.gpsimd.tensor_tensor(gb[:, 2, i, :].rearrange("p (h n) -> p h n", h=2 * H), q, q, ALU.mult)
                sq.then_inc(nrm_sq, 1)

            pool_rstd(0)
            pool_rstd(1)
            with pool.Fori(2, NG) as g:
                pool_rstd(g)
                squares(g - 2)
            squares(NG - 2)
            squares(NG - 1)
            pool.wait_ge(flag_all, 2)
            nc.gpsimd.partition_all_reduce(small[:, 4:6], small[:, 2:4], P, RMAX).then_inc(flag_all, 1)

            def prep_batch(b, slow):
                t0 = b * TPB

                def chained(ins):
                    prep_count[0] += 1
                    ins.then_inc(prep_c, 1)
                    pool.wait_ge(prep_c, b * PREP_STEPS + prep_count[0])
                    apart(pool)

                prep_count = [0]
                for s, dst in ((0, cq_tok), (1, ck_tok)):
                    src = qk_view(t0, s, NQ, HW)
                    if not (isinstance(b, int) and b == 0):
                        pool.wait_ge(t_ps, (b - 1) * 7 + 2 + 2 * s)
                    a, c, e = (dst[:, :, :, o, :] for o in (1, 0, 2))
                    chained(nc.gpsimd.tensor_copy(a, src))
                    chained(nc.gpsimd.tensor_tensor(scr, src, a, ALU.subtract))
                    chained(nc.gpsimd.tensor_copy(c, scr))
                    nc.gpsimd.tensor_tensor(e, scr, c, ALU.subtract).then_inc(prep, 1)
                    pool.wait_ge(prep, b * 5 + 1 + s)
                if isinstance(b, int) and b == 0:
                    pool.wait_ge(inv_ready, 1)
                for s in (1, 0):
                    src = qk_view(t0, s, 0, NQ)
                    if not (isinstance(b, int) and b == 0):
                        pool.wait_ge(t_ps, (b - 1) * 7 + (6 if s else 7))
                    by = inv[:, bass.ds(t0, TPB), s * H:(s + 1) * H].unsqueeze(3).to_broadcast([P, TPB, H, NQ])
                    chained(nc.gpsimd.tensor_tensor(scr_u, src, by, ALU.mult))
                    if s == 0:
                        parts = uq_tok.rearrange("p t h (r n) -> p (t h) r n", r=2)
                        ub = scr_u.rearrange("p t h n -> p (t h) n").unsqueeze(2).to_broadcast([P, TPB * H, 2, NQ])
                        chained(nc.gpsimd.tensor_copy(parts[:, :, :, 0:NQ], ub))
                        nc.gpsimd.tensor_tensor(parts[:, :, :, NQ:2 * NQ], ub, parts[:, :, :, 0:NQ],
                                                ALU.subtract).then_inc(prep, 1)
                    else:
                        for tt in range(TPB):
                            for g in range(2):
                                flat = uk_tok[:, tt, 4 * g:4 * g + 4, :].rearrange("p h n -> p (h n)")
                                hi = diag_view(flat, 0)
                                lo = diag_view(flat, 2 * NQ)
                                u = scr_u[:, tt, 4 * g:4 * g + 4, :]
                                ub = u.unsqueeze(2).to_broadcast([P, 4, 2, NQ])
                                chained(nc.gpsimd.tensor_copy(hi, ub))
                                last = nc.gpsimd.tensor_tensor(lo, ub, hi, ALU.subtract)
                                if tt == TPB - 1 and g == 1:
                                    last.then_inc(prep, 1)
                                    pool.wait_ge(prep, b * 5 + 3)
                                else:
                                    chained(last)
                return t0

            def diag_view(flat, off):
                v = flat[:, off:off + 1]
                ap = [list(d) for d in v.ap]
                return bass.AP(v.tensor, v.offset, [ap[0], [P + QBLK, 4], [NQ, 2], [1, NQ]])

            PREP_STEPS = 3 + 3 + 1 + 4 + 3 + 2

            def prep_v(b, par):
                if not (isinstance(b, int) and b < 2):
                    pool.wait_ge(pv_done, b)
                v = vbuf[:, par, :, 0:H * VW].rearrange("p t (h n) -> p t h n", h=H)[:, :, :, 0:HD]
                src = proj[:, bass.ds(b * TPB, TPB), 2 * SIDE:PW].rearrange("p t (h n) -> p t h n", h=H)
                nc.gpsimd.tensor_copy(v, src).then_inc(prep, 1)

            def body(b, par, first, last, slow):
                prep_batch(b, slow)
                prep_v(b, par)
            batches(pool, body, False)

            pool.wait_ge(h_done, NB + 1)

            def rstd_c(k, name, n):
                pool.wait_ge(step["var_" + name], n + 1)
                apart(pool)
                nc.gpsimd.tensor_scalar(ln[:, k, :, 8], ln[:, k, :, 7], LN_EPS, None, ALU.add).then_inc(step["e" + name], 1)
                pool.wait_ge(step["e" + name], n + 1)
                nc.gpsimd.tensor_tensor(ln[:, k, :, 9], ln[:, k, :, 8], mhalf[:, 0:GT], ALU.pow).then_inc(step["r_" + name], 1)

            def xnb(g):
                if not (isinstance(g, int) and g == 0):
                    pool.wait_ge(step["y"], g)
                nc.gpsimd.tensor_copy(xnb4, x_all[:, bass.ds(g * GT, GT), :]).then_inc(step["nb"], 1)
                pool.wait_ge(step["nb"], 2 * g + 1)
                apart(pool)
                for i in range(GT):
                    ts = nc.gpsimd.tensor_scalar(xnb4[:, i, :], xnb4[:, i, :], xstat[:, 0, i:i + 1], xstat[:, 1, i:i + 1],
                                                 ALU.subtract, ALU.mult)
                ts.then_inc(step["nb"], 1)
                pool.wait_ge(step["nb"], 2 * g + 2)
                nc.gpsimd.tensor_tensor(xnb4, xnb4, bo_bc.unsqueeze(1).to_broadcast([P, GT, C]), ALU.add).then_inc(step["xnb"], 1)

            def xstats(g):
                nc.gpsimd.tensor_copy(xstat[:, :, :], mv_all[:, :, bass.ds(g * GT, GT)]).then_inc(step["na"], 1)
                pool.wait_ge(step["na"], g + 1)

            def c_body(g, one_, two, more):
                if one_:
                    rstd_c(0, "a", g)
                if two:
                    rstd_c(1, "b", g - 1)
                if two:
                    rstd_c(2, "c", g - 1)
                    rstd_c(3, "d", g - 1)
                    pool.wait_ge(step["xr"], g)
                    nc.gpsimd.tensor_copy(proj[:, bass.ds((g - 1) * GT, GT), 0:C], xr4)
                    nc.gpsimd.tensor_copy(proj[:, bass.ds((g - 1) * GT, GT), 2 * C + 1], tok_id[:, bass.ds((g - 1) * GT, GT)]).then_inc(step["rows"], 1)
                if more:
                    xstats(g + 1)
                    xnb(g + 1)

            xstats(0)
            xnb(0)
            c_loop(pool, c_body)

            pool.wait_ge(rsem["i"], 1)
            pool.wait_ge(step["rows"], NG + 1)
            pool.wait_ge(z_stored, 64)
            for t in range(NT):
                nc.gpsimd.indirect_dma_start(xs_d, bass.IndirectOffsetOnAxis(ap=sl_i[:, t:t + 1], axis=0),
                                             proj[:, t, 0:ROW], None).then_inc(scat, 16)

            out2 = out.rearrange("b s c -> (b s) c")

            def f_rstd(i, j):
                s = DEPTH * i + j
                par = j % 2
                pool.wait_ge(fs["var"], s + 1)
                apart(pool)
                nc.gpsimd.tensor_scalar(fst[:, par, :, 8], fst[:, par, :, 7], LN_EPS, None, ALU.add).then_inc(fs["veps"], 1)
                pool.wait_ge(fs["veps"], s + 1)
                nc.gpsimd.tensor_tensor(fst[:, par, :, 9], fst[:, par, :, 8], mhalf[:, 0:RS], ALU.pow).then_inc(fs["r"], 1)

            def f_store(i, j):
                s = DEPTH * i + j
                pool.wait_ge(fs["idx"], s + 1)
                pool.wait_ge(fs["res"], s + 1)
                apart(pool)
                for t in range(RS):
                    nc.gpsimd.indirect_dma_start(out2, bass.IndirectOffsetOnAxis(ap=fidx[:, j, t:t + 1], axis=0),
                                                 fres[j][:, t, :], None, bounds_check=NT * P - 1,
                                                 oob_is_err=False).then_inc(f_out[j], 16)

            def f_body(i, j):
                f_rstd(i, j)
                before = after(i, j, -1)
                if exists(*before):
                    f_store(*before)

            f_loop(pool, f_body)
            f_store(NS // DEPTH - 1, DEPTH - 1)

        @block.scalar
        def _(act):
            act.sem_inc(xnT_ready, 1)
            for i, w in enumerate((Wq, Wk, Wv)):
                act.dma_start(wraw[:, i, :].rearrange("p (h d) -> p h d", h=H), w.rearrange("h c d -> c h d")).then_inc(qkv_loaded, 16)
            for i, v in enumerate((bq, bk)):
                act.dma_start(bcol[:, i:i + 1], v.rearrange("h (d a) -> (h d) a", a=1)).then_inc(qkv_loaded, 16)
                act.dma_start(qb_bc[:, i, :], v.rearrange("h d -> (h d)").partition_broadcast(P)).then_inc(qkv_loaded, 16)
            act.dma_start(bias_bc[:, 2 * SIDE:PW], bv.rearrange("h d -> (h d)").partition_broadcast(P)).then_inc(qkv_loaded, 16)
            act.dma_start(bc2q_bc[:, :], bc2q.rearrange("h n -> (h n)").partition_broadcast(P)).then_inc(qkv_loaded, 16)
            act.wait_ge(set_pe, 1)
            nc.scalar.copy(wT[:, :, :].rearrange("p a n -> p (a n)"), ps[:, 4, 0:2 * P]).then_inc(set_cp, 1)
            with act.Fori(0, NG) as g:
                act.wait_ge(xnT_ps, g + 2)
                act.wait_ge(proj_ps, g * GT + 1)
                nc.scalar.copy(gb[:, 1, :, :].rearrange("p t n -> p (t n)"), tbank).then_inc(xnT_ready, 1)
            act.wait_ge(nrm, 1)
            n2f = n2[:, :, :].rearrange("p t h -> p (t h)")
            nc.scalar.activation(inv[:, :, :].rearrange("p t h -> p (t h)"), n2f, ACT.Sqrt).then_inc(nrm_root, 1)

            def body(b, par, first, last, slow):
                def sin(n):
                    if slow:
                        act.wait_ge(g_f, b * HP + n + 1)
                        src = g_cos
                    else:
                        act.wait_ge(unit_ready, 3 * HP * b + HP + n + 1)
                        src = slot[(HP + n) % 3]
                    if n == 0 and not (isinstance(b, int) and b < 2):
                        act.wait_ge(pv_done, b)
                    nc.scalar.activation(W[par][:, n, :], src, ACT.Sin, scale=PI * (1 - 1e-6)).then_inc(sin_ready, 1)

                def evac(n, b1, par1):
                    act.wait_ge(t_ps, 7 * b1 + n + 1)
                    dst, src = t_dst(par1, n)
                    nc.scalar.copy(dst, src).then_inc(t_act, 1)

                def nxt(n):
                    if not last:
                        evac(n, b + 1, 1 - par)

                if first:
                    evac(0, 0, 0)
                    evac(2, 0, 0)
                    evac(4, 0, 0)
                evac(5, b, par)
                evac(6, b, par)
                for n in range(HP):
                    sin(n)
                nxt(0)
                for n in range(HP):
                    act.wait_ge(z_ready, HP * b + n + 1)
                    nc.scalar.activation(W[par][:, n, :], W[par][:, n, :], ACT.Exp).then_inc(p_ready, 1)
                    if n == 0 and not first:
                        act.wait_ge(pv_done, b + 1)
                        act.wait_ge(h_tr, b)
                        nc.scalar.copy(hT[:, :], hbank).then_inc(h_sb, 1)
                    if n in (1, 2):
                        nxt(2 * n)
                if last:
                    act.wait_ge(pv_done, b + 2)
                    act.wait_ge(h_tr, b + 1)
                    nc.scalar.copy(hT[:, :], hbank).then_inc(h_sb, 1)

            act.wait_ge(z_stored, 64)
            either(act, body)

            def flat(v):
                return v.rearrange("p t n -> p (t n)")

            def copy_at(g):
                if not (isinstance(g, int) and g == 0):
                    act.wait_ge(step["at_ps"], g)
                nc.scalar.copy(at4, proj[:, bass.ds(g * GT, GT), 0:C]).then_inc(step["at"], 1)

            def c_body(g, one_, two, more):
                if more:
                    copy_at(g + 1)
                if one_:
                    act.wait_ge(step["x1_ps"], g + 1)
                    nc.scalar.copy(flat(x1T4), ps[:, 2, :]).then_inc(step["x1T"], 1)
                    act.wait_ge(step["v0"], g + 1)
                    nc.scalar.activation(qm[:, 2, :, :], qm[:, 0, :, :], ACT.Tanh).then_inc(step["tanh"], 1)
                if more:
                    copy_aT(g + 1)
                if one_:
                    act.wait_ge(step["ang"], g + 1)
                    nc.scalar.activation(qm[:, 3, :, :], qm[:, 1, :, :], ACT.Sin, bias=halfpi[:, 0:1], scale=-2 * PI).then_inc(step["cos"], 1)
                    act.wait_ge(step["qe_ps"], g + 1)
                    nc.scalar.copy(qeT[:, :], ps[0:NQ + 1, 4, :]).then_inc(step["qeT"], 1)
                if two:
                    act.wait_ge(step["xr_ps"], g)
                    nc.scalar.copy(flat(xrT4), ps[:, 6, :]).then_inc(step["xrT"], 1)

            def copy_aT(g):
                act.wait_ge(step["at_ps"], g + 1)
                if not (isinstance(g, int) and g == 0):
                    act.wait_ge(step["wo_ps"], g)
                nc.scalar.copy(flat(aT4), ps[:, 0, :]).then_inc(step["aT"], 1)

            act.wait_ge(h_done, NB + 1)
            copy_at(0)
            copy_aT(0)
            c_loop(act, c_body)

            act.wait_ge(rsem["e"], 1)
            nc.scalar.activation(rt[:, 1, :, :], rt[:, 1, :, :], ACT.Exp).then_inc(rsem["s"], 1)

            def f_xT(i, j):
                act.wait_ge(fs["xT_ps"], DEPTH * i + j + 1)
                nc.scalar.copy(fxT[j % 2], ps[:, 0, 0:TS]).then_inc(fs["xT"], 1)

            def f_body(i, j):
                s = DEPTH * i + j
                par = j % 2
                for c in range(EC):
                    if c % 2 == 0:
                        act.wait_ge(fs["h_ps"], s * (EC // 2) + c // 2 + 1)
                    bias = fbias[:, s, c:c + 1] if isinstance(s, int) else fbias[:, bass.ds(s, 1), c:c + 1].rearrange("p s c -> p (s c)")
                    nc.scalar.activation(fg[par][:, c, :], ps[:, 1 + 2 * par + c // 2, (c % 2) * TS:(c % 2 + 1) * TS], ACT.Gelu,
                                         bias=bias).then_inc(fs["g"], 1)
                if exists(*after(i, j, 2)):
                    f_xT(*after(i, j, 2))
                act.wait_ge(fs["y_ps"], s + 1)
                bias = fbias[:, s, EC:EC + 1] if isinstance(s, int) else fbias[:, bass.ds(s, 1), EC:EC + 1].rearrange("p s c -> p (s c)")
                nc.scalar.activation(fyT[par], ps[:, 5 + 2 * par, 0:TS], ACT.Identity, bias=bias).then_inc(fs["yT"], 1)

            f_xT(0, 0)
            f_xT(0, 1)
            act.wait_ge(fs["bias"], 1)
            f_loop(act, f_body)

        @block.tensor
        def _(pe):
            pe.sem_inc(xnT_ps, 1)
            pe.sem_inc(proj_ps, 1)
            pe.sem_inc(pv_done, 1)
            pe.sem_inc(h_tr, 1)
            pe.wait_ge(consts_ready, 4)
            pe.wait_ge(qkv_loaded, 16 * 9)
            for i in range(2):
                mm = nc.tensor.transpose(ps[:, 4, i * P:(i + 1) * P], wraw[:, i, :], ident[:, :])
            mm.then_inc(set_pe, 1)
            pe.wait_ge(set_cp, 2)
            pe.wait_ge(bd_loaded, 16 * H)
            w = H * NQ
            for i in range(2):
                nc.tensor.matmul(ps[:, 5, i * w:(i + 1) * w], wT[:, i, :], bdiag[:, :], start=True, stop=True)
            for i in range(2):
                mm = nc.tensor.matmul(ps[:, 5, (2 + i) * w:(3 + i) * w], bcol_bc[:, i, :], bdiag[:, :], start=True, stop=True)
            mm.then_inc(set_pe, 1)
            with pe.Fori(0, NG) as g:
                pe.wait_ge(xn_ready, g + 1)
                pe.wait_ge(xnT_ready, g + 1)
                for i in range(GT):
                    mm = nc.tensor.transpose(tbank[:, i * P:(i + 1) * P], gb[:, 0, i, :], ident[:, :])
                mm.then_inc(xnT_ps, 1)
                pe.wait_ge(xnT_ready, g + 2)
                pe.wait_ge(wcat_ready, 1)
                for i in range(GT):
                    pe.wait_ge(proj_ready, g * GT + i + 1)
                    nc.tensor.matmul(ps[:, i, :], gb[:, 1, i, :], wcat[:, :], start=True, stop=True).then_inc(proj_ps, 1)
            pe.wait_ge(post_loaded, 16 * 17)
            pe.wait_ge(consts_ready, 16)
            pe.wait_ge(proj_ready, NT + GT)
            for i in range(FC):
                nc.tensor.transpose(ps[:, 0, i * P:(i + 1) * P], w1_sb[:, i * P:(i + 1) * P], ident[:, :])
            for i in range(FC):
                mm = nc.tensor.transpose(ps[:, 1, i * 16:i * 16 + NQ + 1], wqo9[:, i * P:(i + 1) * P],
                                         ident[0:NQ + 1, 0:NQ + 1])
            mm.then_inc(set_pe, 1)
            pe.wait_ge(set_cp, 4)
            for i in range(FC):
                nc.tensor.matmul(ps[:, 2, 0:NQ], w1T[:, i, :], wm_sb[:, i, :], start=(i == 0), stop=(i == FC - 1))
            for i in range(FC):
                nc.tensor.matmul(ps[:, 3, 0:NQ], b1c_bc[:, i, :], wm_sb[:, i, :], start=(i == 0), stop=False)
            nc.tensor.matmul(ps[:, 3, 0:NQ], one[:, :], bm_row[:, :], start=False, stop=True)
            for i in range(FC):
                nc.tensor.matmul(ps[0:NQ + 1, 4, 0:C], wqoT[:, i, :], w2_sb[:, i, :], start=(i == 0), stop=False)
            nc.tensor.matmul(ps[0:NQ + 1, 4, 0:C], e9[:, :], b2_row[:, :], start=False, stop=True).then_inc(set_pe, 1)
            pe.wait_ge(set_cp, 7)

            def body(b, par, first, last, slow):
                def scores(k):
                    if 3 <= k < 2 * HP + 3:
                        pe.wait_ge(unit_free, 2 * HP * b + k - 2)
                    elif k >= 2 * HP + 3:
                        pe.wait_ge(z_ready, HP * b + k - 2 * HP - 2)
                    elif not first:
                        pe.wait_ge(z_ready, HP * b + k - 2)
                    return slot[k % 3]

                def guard_unit(n):
                    pe.wait_ge(g_mask, HP * b + n + 1)
                    o = scores(HP + n + 1)
                    for h in range(2):
                        for kt in range(TPB):
                            c = (h * TPB + kt) * S
                            mm = nc.tensor.matmul(o[:, c:c + S], g_row[:, S + kt * P:S + (kt + 1) * P],
                                                  g_qrow[:, h * S:(h + 1) * S], start=True, stop=True)
                    mm.then_inc(g_ps, 1)
                    pe.wait_ge(g_min, HP * b + n + 1)

                def norm_rows():
                    pe.wait_ge(g_src, b + 1)
                    bank_free(b, 5)
                    for s in range(2):
                        for tt in range(TPB):
                            c = s * S + tt * P
                            mm = nc.tensor.transpose(tbank[0:H, c:c + P], g_norm[:, tt, s * H:(s + 1) * H], ident[:, :])
                    mm.then_inc(g_tr, 1)
                    pe.wait_ge(g_rows, b + 1)

                def max_unit(n):
                    o = scores(n)
                    for h in range(2):
                        for qt in range(TPB):
                            c = (h * TPB + qt) * S
                            mm = nc.tensor.matmul(o[:, c:c + S], cqT[par][0:KC, 2 * n + h, qt * P:(qt + 1) * P],
                                                  ckT[par][0:KC, 2 * n + h, :], start=True, stop=True)
                    mm.then_inc(unit_ready, 1)

                def cos_unit(n):
                    o = scores(HP + n)
                    for h in range(2):
                        for kt in range(TPB):
                            c = (h * TPB + kt) * S
                            mm = nc.tensor.matmul(o[:, c:c + S], ukT[par][:, 2 * n + h, kt * P:(kt + 1) * P],
                                                  uqT[par][:, n // 2, :], start=True, stop=True)
                    mm.then_inc(unit_ready, 1)
                    if slow:
                        guard_unit(n)

                def logit_unit(n):
                    o = scores(2 * HP + n)
                    for h in range(2):
                        for kt in range(TPB):
                            c = (h * TPB + kt) * S
                            mm = nc.tensor.matmul(o[:, c:c + S], ckT[par][0:KC + 2, 2 * n + h, kt * P:(kt + 1) * P],
                                                  cqT[par][0:KC + 2, 2 * n + h, :], start=True, stop=True)
                    mm.then_inc(unit_ready, 1)

                def trans(n, b1):
                    pe.wait_ge(prep, b1 * 5 + [1, 1, 2, 2, 3, 3, 4][n])
                    bank_free(b1, n)
                    if n == 0 and not (isinstance(b1, int) and b1 == 0):
                        pe.wait_ge(m_T, 2 * b1)
                    for tt in range(TPB):
                        if n < 4:
                            for h in range(4):
                                for i in range(3):
                                    blk = (cq_block if n < 2 else ck_block)(tt, 4 * (n % 2) + h, i)
                                    c = h * S + tt * P
                                    mm = nc.tensor.transpose(tb[32 * i:32 * i + 32, c:c + P], blk, ident_b[:, :])
                        elif n < 6:
                            for h in range(4):
                                c = h * S + tt * P
                                mm = nc.tensor.transpose(th[:, c:c + P], uk_tok[:, tt, 4 * (n - 4) + h, :], ident_h[:, :])
                        else:
                            for g in range(2):
                                c = g * S + tt * P
                                mm = nc.tensor.transpose(th[:, c:c + P], uq_block(tt, g), ident_h[:, :])
                    mm.then_inc(t_ps, 1)

                def bank_free(b1, n):
                    a, d = act_before(b1, n), dve_before(b1, n)
                    if not (isinstance(a, int) and a == 0):
                        pe.wait_ge(t_act, a)
                    if not (isinstance(d, int) and d == 0):
                        pe.wait_ge(t_dve, d)

                def nxt(n):
                    if not last:
                        trans(n, b + 1)

                def maxima(r):
                    pe.wait_ge(m_tok, b + 1)
                    if r == 0:
                        bank_free(b + 1, 0)
                    else:
                        pe.wait_ge(m_T, 2 * b + 1)
                    for h in range(4):
                        for qt in range(TPB):
                            c = h * S + qt * P
                            mm = nc.tensor.transpose(tb[96:98, c:c + P], mtok[:, qt, 4 * r + h, :], ident_b[:, :])
                    mm.then_inc(m_ps, 1)

                def pv(b1, par1, g):
                    if g == 0:
                        pe.wait_ge(p_ready, HP * (b1 + 1))
                        pe.wait_ge(prep, b1 * 5 + 5)
                        pe.wait_ge(h_done, b1 + 1)
                    for kt in range(TPB):
                        for j in range(4):
                            h = 4 * g + j
                            c = ((h % 2) * TPB + kt) * S
                            mm = nc.tensor.matmul(hbank[32 * j:32 * j + 32, g * S:(g + 1) * S],
                                                  vbuf[:, par1, kt, h * VW:h * VW + 32],
                                                  W[par1][:, h // 2, c:c + S], start=(kt == 0), stop=(kt == 1),
                                                  skip_group_check=True)
                    if g == 1:
                        mm.then_inc(pv_done, 1)

                def heads_back(b1):
                    pe.wait_ge(h_sb, b1 + 1)
                    for tt in range(TPB):
                        for g in range(2):
                            c = (tt * 2 + g) * P
                            mm = nc.tensor.transpose(hbank[:, c:c + P], hT[:, g * S + tt * P:g * S + (tt + 1) * P], ident[:, :])
                    mm.then_inc(h_tr, 1)

                if first:
                    for n in range(5):
                        trans(n, 0)
                pe.wait_ge(t_act, act_before(b, 4))
                pe.wait_ge(t_dve, dve_before(b, 4))
                if slow:
                    norm_rows()
                max_unit(0)
                trans(5, b)
                max_unit(1)
                max_unit(2)
                trans(6, b)
                max_unit(3)
                pe.wait_ge(t_act, act_before(b + 1, 0))
                pe.wait_ge(t_dve, dve_before(b + 1, 0))
                if slow:
                    maxima(0)
                    maxima(1)
                cos_unit(0)
                cos_unit(1)
                cos_unit(2)
                if not slow:
                    maxima(0)
                    maxima(1)
                if not first:
                    pv(b - 1, 1 - par, 0)
                cos_unit(3)
                nxt(0)
                pe.wait_ge(m_T, 2 * b + 2)
                logit_unit(0)
                nxt(1)
                logit_unit(1)
                if not first:
                    pv(b - 1, 1 - par, 1)
                nxt(2)
                logit_unit(2)
                if not first:
                    heads_back(b - 1)
                nxt(3)
                logit_unit(3)
                nxt(4)
                if last:
                    pv(b, par, 0)
                    pv(b, par, 1)
                    heads_back(b)

            either(pe, body)

            def turned(bank, src, n=GT):
                for i in range(n):
                    mm = nc.tensor.transpose(bank[:, i * P:(i + 1) * P], src[:, i, :], ident[:, :])
                return mm

            def c_body(g, one_, two, more):
                if one_:
                    pe.wait_ge(step["x1"], g + 1)
                    turned(ps[:, 2, :], x14).then_inc(step["x1_ps"], 1)
                    pe.wait_ge(step["x1T"], g + 1)
                    for i in range(GT):
                        mm = nc.tensor.matmul(ps[:, 3, i * NQ:(i + 1) * NQ], x1T4[:, i, :], wA[:, :], start=True, stop=True)
                    mm.then_inc(step["qm_ps"], 1)
                if more:
                    project_heads(g + 1)
                if one_:
                    pe.wait_ge(step["qe"], g + 1)
                    for i in range(GT):
                        mm = nc.tensor.transpose(ps[0:NQ + 1, 4, i * P:(i + 1) * P], qe[:, i, :], ident[:, :])
                    mm.then_inc(step["qe_ps"], 1)
                    pe.wait_ge(step["qeT"], g + 1)
                    if two:
                        pe.wait_ge(step["y2"], g)
                    for i in range(GT):
                        mm = nc.tensor.matmul(ps[:, 5, i * P:(i + 1) * P], qeT[:, i * P:(i + 1) * P], wB[:, :], start=True, stop=True)
                    mm.then_inc(step["ff_ps"], 1)
                if two:
                    pe.wait_ge(step["xr"], g)
                    turned(ps[:, 6, :], xr4).then_inc(step["xr_ps"], 1)
                    pe.wait_ge(step["xrT"], g)
                    for i in range(GT):
                        mm = nc.tensor.matmul(ps[:, 7, i * NE:(i + 1) * NE], xrT4[:, i, :], gw_sb[:, :], start=True, stop=True)
                    mm.then_inc(step["lg_ps"], 1)

            def project_heads(g):
                pe.wait_ge(step["at"], g + 1)
                turned(ps[:, 0, :], at4).then_inc(step["at_ps"], 1)
                pe.wait_ge(step["aT"], g + 1)
                if not (isinstance(g, int) and g == 0):
                    pe.wait_ge(step["y"], g)
                for i in range(GT):
                    mm = nc.tensor.matmul(ps[:, 1, i * P:(i + 1) * P], aT4[:, i, :], wo_sb[:, :], start=True, stop=True)
                mm.then_inc(step["wo_ps"], 1)

            pe.wait_ge(h_done, NB + 1)
            project_heads(0)
            c_loop(pe, c_body)

            pe.wait_ge(rsem["p"], 1)
            m = rt[:, 0, :, :].rearrange("p t e -> p (t e)")
            nc.tensor.matmul(ps[:, 0, 0:NT * NE], tri[:, :], m, start=True, stop=True)
            nc.tensor.matmul(ps[:, 1, 0:NT * NE], ones[:, :], m, start=True, stop=True).then_inc(rsem["p"], 1)

            def f_in(i, j):
                s = DEPTH * i + j
                pe.wait_ge(f_rows[j], 16 * (i + 1))
                if exists(*after(i, j, -1)):
                    pe.wait_ge(fs["xT"], s)
                for t in range(RS):
                    mm = nc.tensor.transpose(ps[:, 0, t * P:(t + 1) * P], frow[j][:, t, 0:C], ident[:, :])
                mm.then_inc(fs["xT_ps"], 1)

            def f_up(i, j):
                s = DEPTH * i + j
                par = j % 2
                pe.wait_ge(f_w[j], 32 * (i + 1))
                pe.wait_ge(fs["xT"], s + 1)
                for c in range(EC):
                    mm = nc.tensor.matmul(ps[:, 1 + 2 * par + c // 2, (c % 2) * TS:(c % 2 + 1) * TS],
                                          fw1[j][:, c * P:(c + 1) * P], fxT[par], start=True, stop=True)
                    if c % 2 == 1:
                        mm.then_inc(fs["h_ps"], 1)

            def f_down(i, j):
                s = DEPTH * i + j
                par = j % 2
                for c in range(EC):
                    pe.wait_ge(fs["g"], s * EC + c + 1)
                    mm = nc.tensor.matmul(ps[:, 5 + 2 * par, 0:TS], fw2[j][:, c, :], fg[par][:, c, :], start=(c == 0), stop=(c == EC - 1))
                mm.then_inc(fs["y_ps"], 1)

            def f_back(i, j):
                s = DEPTH * i + j
                pe.wait_ge(fs["yT"], s + 1)
                if exists(*after(i, j, -1)):
                    pe.wait_ge(fs["wy"], s)
                for t in range(RS):
                    mm = nc.tensor.transpose(ps[:, 6, t * P:(t + 1) * P], fyT[j % 2][:, t * P:(t + 1) * P], ident[:, :])
                mm.then_inc(fs["y_tr"], 1)

            def f_body(i, j):
                if exists(*after(i, j, 1)):
                    f_up(*after(i, j, 1))
                if exists(*after(i, j, -1)):
                    f_back(*after(i, j, -1))
                if exists(*after(i, j, 2)):
                    f_in(*after(i, j, 2))
                f_down(i, j)

            f_in(0, 0)
            f_up(0, 0)
            f_in(0, 1)
            f_loop(pe, f_body)
            f_back(NS // DEPTH - 1, DEPTH - 1)

        @block.vector
        def _(dve):
            dve.sem_inc(nrm_red, 1)
            dve.sem_inc(h_done, 1)
            nc.vector.memset(bigf[:, 0:NS * TS * ROW // P // 4], 0.0).then_inc(zfill, 1)
            def ln_stats(g):
                for i in range(GT):
                    bs = nc.vector.bn_stats(stats[:, i, :], x_all[:, bass.ds(g * GT + i, 1), :].rearrange("p t c -> p (t c)"))
                bs.then_inc(st_dve, 1)
                dve.wait_ge(st_dve, 2 * g + 1)
                apart(dve)
                for i in range(GT):
                    ag = nc.vector.bn_aggr(mv[:, i, :], stats[:, i, :])
                ag.then_inc(st_dve, 1)
                dve.wait_ge(st_dve, 2 * g + 2)
                nc.vector.tensor_copy(mv_all[:, 0, bass.ds(g * GT, GT)], mv[:, :, 0])
                nc.vector.tensor_scalar(mv_all[:, 1, bass.ds(g * GT, GT)], mv[:, :, 1], LN_EPS, None, ALU.add).then_inc(st_var, 1)
                dve.wait_ge(st_var, g + 1)

            dve.wait_ge(x_loaded[0], 16)
            ln_stats(0)
            dve.wait_ge(qkv_loaded, 16 * 9)
            for i in range(2):
                cp = nc.vector.tensor_copy(bcol_bc[:, i, :], bcol[:, i:i + 1].to_broadcast([P, P]))
            cp.then_inc(set_cp, 1)
            wq_v = wcat[:, 0:2 * SIDE].rearrange("p (a h n) -> p a h n", a=2, h=H)
            bq_v = bias_bc[:, 0:2 * SIDE].rearrange("p (a h n) -> p a h n", a=2, h=H)
            scale = [0.5 / HD ** 0.5, 1.0]
            for i in range(2):
                nc.vector.tensor_scalar(wq_v[:, i, :, NQ:HW], wraw[:, i, :].rearrange("p (h d) -> p h d", h=H),
                                        scale[i], None, ALU.mult)
                nc.vector.tensor_scalar(bq_v[:, i, :, NQ:HW], qb_bc[:, i, :].rearrange("p (h d) -> p h d", h=H),
                                        scale[i], None, ALU.mult)
            nc.vector.tensor_copy(wcat[:, 2 * SIDE:PW], wraw[:, 2, :])
            dve.wait_ge(set_pe, 2)
            w = H * NQ
            for i in range(2):
                nc.vector.tensor_copy(wq_v[:, i, :, 0:NQ], ps[:, 5, i * w:(i + 1) * w].rearrange("p (h n) -> p h n", h=H))
                last = nc.vector.tensor_tensor(bq_v[:, i, :, 0:NQ], ps[:, 5, (2 + i) * w:(3 + i) * w].rearrange("p (h n) -> p h n", h=H),
                                               bc2q_bc[:, :].rearrange("p (h n) -> p h n", h=H), ALU.add)
            last.then_inc(wcat_ready, 1)
            dve.sem_inc(proj_ready, GT)

            def proj_out(g):
                for i in range(GT):
                    dve.wait_ge(proj_ps, g * GT + i + 2)
                    nc.vector.tensor_tensor(proj[:, bass.ds(g * GT + i, 1), :].rearrange("p t n -> p (t n)"), ps[:, i, :],
                                            bias_bc[:, :], ALU.add).then_inc(proj_ready, 1)

            def norm_out(g):
                dve.wait_ge(nrm_sq, g + 1)
                nc.vector.tensor_reduce(n2[:, bass.ds(g * GT, GT), :].rearrange("p t h -> p (t h)"),
                                        gb[:, 2, :, :].rearrange("p t (h n) -> p (t h) n", h=2 * H), AX_X, ALU.add).then_inc(nrm_red, 1)

            def x_norm(g):
                dve.wait_ge(st_rstd, g + 1)
                dve.wait_ge(xnT_ps, g + 1)
                for i in range(GT):
                    t = g * GT + i
                    xn = nc.vector.tensor_scalar(gb[:, 0, i, :], x_all[:, bass.ds(t, 1), :].rearrange("p t c -> p (t c)"),
                                                 mv_all[:, 0, bass.ds(t, 1)], mv_all[:, 1, bass.ds(t, 1)], ALU.subtract, ALU.mult)
                xn.then_inc(xn_ready, 1)

            x_norm(0)
            for i in range(1, 4):
                dve.wait_ge(x_loaded[i], 16)
            ln_stats(1)
            x_norm(1)
            ln_stats(2)
            proj_out(0)
            with dve.Fori(2, NG - 1) as g:
                x_norm(g)
                ln_stats(g + 1)
                norm_out(g - 2)
                proj_out(g - 1)
            x_norm(NG - 1)
            norm_out(NG - 3)
            proj_out(NG - 2)
            norm_out(NG - 2)
            proj_out(NG - 1)
            norm_out(NG - 1)
            dve.wait_ge(nrm_red, NG + 1)
            n2f = n2[:, :, :].rearrange("p t h -> p (t h)")
            for s in range(2):
                mn = nc.vector.tensor_reduce(small[:, s:s + 1], n2[:, :, s * H:(s + 1) * H], AX_XY, ALU.min)
            mn.then_inc(flag_all, 1)
            dve.wait_ge(flag_all, 1)
            nc.vector.tensor_scalar(small[:, 2:4], small[:, 0:2], -1.0, None, ALU.mult).then_inc(flag_all, 1)
            nc.vector.tensor_scalar(n2f, n2f, 2e-35, None, ALU.max).then_inc(nrm, 1)
            dve.wait_ge(post_loaded, 16 * 17)
            nc.vector.tensor_copy(b1c_bc[:, :, :], b1c[:, :].unsqueeze(2).to_broadcast([P, FC, P]))
            dve.wait_ge(set_pe, 3)
            nc.vector.tensor_copy(w1T[:, :, :].rearrange("p c n -> p (c n)"), ps[:, 0, :]).then_inc(set_cp, 1)
            nc.vector.tensor_copy(wqoT[:, :, :], ps[:, 1, 0:FC * 16].rearrange("p (c n) -> p c n", n=16)[:, :, 0:NQ + 1]).then_inc(set_cp, 1)
            invf = inv[:, :, :].rearrange("p t h -> p (t h)")
            y2 = gb[:, 3, :, :].rearrange("p t n -> p (t n)")
            dve.wait_ge(nrm_root, 1)
            nc.vector.reciprocal(invf, invf).then_inc(nrm, 1)
            dve.wait_ge(nrm, 2)
            nc.vector.tensor_tensor(y2, invf, invf, ALU.mult).then_inc(nrm, 1)
            dve.wait_ge(nrm, 3)
            nc.vector.tensor_tensor(y2, y2, n2f, ALU.mult).then_inc(nrm, 1)
            dve.wait_ge(nrm, 4)
            nc.vector.tensor_scalar(y2, y2, -0.5, 1.5, ALU.mult, ALU.add).then_inc(nrm, 1)
            dve.wait_ge(nrm, 5)
            nc.vector.tensor_tensor(invf, invf, y2, ALU.mult).then_inc(inv_ready, 1)
            dve.wait_ge(flag_all, 3)
            nc.vector.tensor_tensor(small[:, 6:7], small[:, 4:5], small[:, 5:6], ALU.mult).then_inc(flag_all, 1)
            dve.wait_ge(flag_all, 4)
            nc.vector.tensor_scalar(flag[:, :], small[:, 6:7], 1.001 * EPS_COS ** 2, None, ALU.is_lt).then_inc(flag_ready, 1)
            dve.wait_ge(set_pe, 4)
            nc.vector.tensor_copy(wA[:, :], ps[:, 2, 0:NQ]).then_inc(set_cp, 1)
            nc.vector.tensor_copy(bA_bc[:, :], ps[:, 3, 0:NQ]).then_inc(set_cp, 1)
            nc.vector.tensor_copy(wB[:, :], ps[0:NQ + 1, 4, 0:C]).then_inc(set_cp, 1)
            for i in range(2):
                cp = nc.vector.memset(ckT[i][96:98, :, :], 1.0)
            cp.then_inc(t_dve, 1)

            def body(b, par, first, last, slow):
                def top(n):
                    if slow and n == 0:
                        norms()
                    dve.wait_ge(unit_ready, 3 * HP * b + n + 1)
                    src = slot[n % 3].rearrange("p (h t k) -> p t h k", h=2, t=TPB)
                    nc.vector.tensor_reduce(mxs[:, :, 2 * n:2 * n + 2], src, AX_X, ALU.max).then_inc(unit_free, 1)

                def weight(n):
                    f = slot[(HP + n) % 3]
                    if slow:
                        mask(n)
                        guard(n)
                    dve.wait_ge(sin_ready, HP * b + n + 1)
                    if slow:
                        f = g_cos
                    nc.vector.scalar_tensor_tensor(W[par][:, n, :], W[par][:, n, :], 10.0, f, ALU.add, ALU.mult).then_inc(unit_free, 1)

                def norms():
                    t0 = b * TPB
                    nc.vector.scalar_tensor_tensor(g_norm, n2[:, bass.ds(t0, TPB), :], EPS_COS ** -0.5, inv[:, bass.ds(t0, TPB), :],
                                                   ALU.mult, ALU.mult).then_inc(g_src, 1)
                    dve.wait_ge(g_tr, b + 1)
                    nc.vector.tensor_copy(g_row, tbank[0:H, :]).then_inc(g_rows, 1)
                    dve.wait_ge(g_rows, b + 1)

                def mask(n):
                    for h in range(2):
                        mk = nc.vector.tensor_scalar(g_qrow[:, h * S:(h + 1) * S], g_row[:, 0:S],
                                                     ident[0:H, 2 * n + h:2 * n + h + 1], None, ALU.mult)
                    mk.then_inc(g_mask, 1)

                def guard(n):
                    dve.wait_ge(g_ps, HP * b + n + 1)
                    nc.vector.tensor_scalar(g_cos, slot[(HP + n + 1) % 3], 1.0, None, ALU.min).then_inc(g_min, 1)
                    dve.wait_ge(g_min, HP * b + n + 1)
                    nc.vector.tensor_tensor(g_cos, g_cos, slot[(HP + n) % 3], ALU.mult).then_inc(g_f, 1)
                    dve.wait_ge(g_f, HP * b + n + 1)

                def logits(n):
                    k = 2 * HP + n
                    dve.wait_ge(unit_ready, 3 * HP * b + k + 1)
                    nc.vector.scalar_tensor_tensor(W[par][:, n, :], W[par][:, n, :], 0.05, slot[k % 3],
                                                   ALU.mult, ALU.add).then_inc(z_ready, 1)

                def evac(n, b1, par1):
                    dve.wait_ge(t_ps, 7 * b1 + n + 1)
                    dst, src = t_dst(par1, n)
                    nc.vector.tensor_copy(dst, src).then_inc(t_dve, 1)

                def nxt(n):
                    if not last:
                        evac(n, b + 1, 1 - par)

                def maxima():
                    dve.wait_ge(unit_free, 2 * HP * b + HP)
                    nc.vector.tensor_scalar(mtok[:, :, :, 0], mxs[:, :, :], -1.0, None, ALU.mult).then_inc(m_part, 1)
                    dve.wait_ge(m_part, b + 1)
                    nc.vector.scalar_tensor_tensor(mtok[:, :, :, 1], mxs[:, :, :], -1.0, mtok[:, :, :, 0],
                                                   ALU.mult, ALU.subtract).then_inc(m_tok, 1)

                def maxima_out(r):
                    dve.wait_ge(m_ps, 2 * b + r + 1)
                    nc.vector.tensor_copy(cqT[par][96:98, 4 * r:4 * r + 4, :].rearrange("p h s -> p (h s)"),
                                          tb[96:98, 0:4 * S]).then_inc(m_T, 1)

                def heads(b1):
                    v = hbank.rearrange("p (t h n) -> p t h n", t=TPB, h=H)
                    dve.wait_ge(h_tr, b1 + 2)
                    nc.vector.reciprocal(hsum[:, :, :], v[:, :, :, HD]).then_inc(h_rec, 1)
                    dve.wait_ge(h_rec, b1 + 1)
                    o = proj[:, bass.ds(b1 * TPB, TPB), 0:C].rearrange("p t (h d) -> p t h d", h=H)
                    nc.vector.tensor_tensor(o, v[:, :, :, 0:HD], hsum[:, :, :].unsqueeze(3).to_broadcast([P, TPB, H, HD]),
                                            ALU.mult).then_inc(h_done, 1)

                if first:
                    evac(1, 0, 0)
                    evac(3, 0, 0)
                top(0)
                top(1)
                top(2)
                top(3)
                maxima()
                maxima_out(0)
                if slow:
                    maxima_out(1)
                weight(0)
                if not slow:
                    maxima_out(1)
                weight(1)
                weight(2)
                weight(3)
                logits(0)
                nxt(1)
                logits(1)
                logits(2)
                nxt(3)
                if not first:
                    heads(b - 1)
                logits(3)
                if last:
                    heads(b)

            either(dve, body)

            dve.wait_ge(h_done, NB + 1)

            def stats_c(k, name, src, n):
                for i in range(GT):
                    bs = nc.vector.bn_stats(ln[:, k, i, 0:6], src(i))
                bs.then_inc(step["st_" + name], 1)
                dve.wait_ge(step["st_" + name], n + 1)
                apart(dve)
                for i in range(GT):
                    ag = nc.vector.bn_aggr(ln[:, k, i, 6:8], ln[:, k, i, 0:6])
                ag.then_inc(step["var_" + name], 1)

            def affine(k, src, dst, gain, shift, own, n):
                for i in range(GT):
                    s1 = nc.vector.scalar_tensor_tensor(src[:, i, :], src[:, i, :], ln[:, k, i, 6:7], gain, ALU.subtract, ALU.mult)
                s1.then_inc(own, 1)
                dve.wait_ge(own, n + 1)
                for i in range(GT):
                    s2 = nc.vector.scalar_tensor_tensor(dst[:, i, :], src[:, i, :], ln[:, k, i, 9:10], shift, ALU.mult, ALU.add)
                return s2

            def c_body(g, one_, two, more):
                if one_:
                    dve.wait_ge(step["wo_ps"], g + 1)
                    dve.wait_ge(step["xnb"], g + 1)
                    nc.vector.tensor_tensor(y4, ps[:, 1, :].rearrange("p (t n) -> p t n", t=GT), xnb4, ALU.add).then_inc(step["y"], 1)
                    dve.wait_ge(step["y"], g + 1)
                    stats_c(0, "a", lambda i: y4[:, i, :], g)
                if two:
                    dve.wait_ge(step["ff_ps"], g)
                    nc.vector.tensor_tensor(yy4, ps[:, 5, :].rearrange("p (t n) -> p t n", t=GT), x14, ALU.add).then_inc(step["y2"], 1)
                    dve.wait_ge(step["y2"], g)
                    stats_c(1, "b", lambda i: yy4[:, i, :], g - 1)
                if one_:
                    dve.wait_ge(step["r_a"], g + 1)
                    affine(0, y4, x14, g1_bc, be1_bc, step["v3"], g).then_inc(step["x1"], 1)
                if two:
                    dve.wait_ge(step["r_b"], g)
                    affine(1, yy4, o4, g2_bc, be2_bc, step["x2a"], g - 1).then_inc(step["o"], 1)
                    dve.wait_ge(step["o"], g)
                    stats_c(2, "c", lambda i: o4[:, i, :], g - 1)
                if one_:
                    dve.wait_ge(step["qm_ps"], g + 1)
                    nc.vector.tensor_tensor(qm[:, 0, :, :], ps[:, 3, 0:GT * NQ].rearrange("p (t n) -> p t n", t=GT),
                                            bA_bc[:, :].unsqueeze(1).to_broadcast([P, GT, NQ]), ALU.add).then_inc(step["v0"], 1)
                    dve.wait_ge(step["v0"], g + 1)
                    nc.vector.tensor_scalar(qm[:, 1, :, :], qm[:, 0, :, :], 0.125, MAGIC, ALU.mult, ALU.add).then_inc(step["v1"], 1)
                    dve.wait_ge(step["v1"], 2 * g + 1)
                    nc.vector.tensor_scalar(qm[:, 1, :, :], qm[:, 1, :, :], -MAGIC, None, ALU.add).then_inc(step["v1"], 1)
                    dve.wait_ge(step["v1"], 2 * g + 2)
                    nc.vector.scalar_tensor_tensor(qm[:, 1, :, :], qm[:, 0, :, :], 0.125, qm[:, 1, :, :], ALU.mult, ALU.subtract).then_inc(step["v2"], 1)
                    dve.wait_ge(step["v2"], 3 * g + 1)
                    nc.vector.scalar_tensor_tensor(qm[:, 1, :, :], qm[:, 1, :, :], -1.0, qm[:, 1, :, :], ALU.mult, ALU.max).then_inc(step["v2"], 1)
                    dve.wait_ge(step["v2"], 3 * g + 2)
                    nc.vector.tensor_scalar(qm[:, 1, :, :], qm[:, 1, :, :], 0.5, None, ALU.min).then_inc(step["ang"], 1)
                    nc.vector.sem_inc(step["v2"], 1)
                if two:
                    dve.wait_ge(step["r_c"], g)
                    for i in range(GT):
                        s1 = nc.vector.tensor_scalar(o4[:, i, :], o4[:, i, :], ln[:, 2, i, 6:7], ln[:, 2, i, 9:10], ALU.subtract, ALU.mult)
                    s1.then_inc(step["nrm_o"], 1)
                    dve.wait_ge(step["nrm_o"], g)
                    t0 = (g - 1) * GT
                    nc.vector.tensor_tensor(proj[:, bass.ds(t0, GT), C:2 * C], o4, x_all[:, bass.ds(t0, GT), :], ALU.add).then_inc(step["x2"], 1)
                if one_:
                    dve.wait_ge(step["tanh"], g + 1)
                    dve.wait_ge(step["cos"], g + 1)
                    nc.vector.tensor_tensor(qe[:, :, 0:NQ], qm[:, 2, :, :], qm[:, 3, :, :], ALU.mult).then_inc(step["qe"], 1)
                if two:
                    dve.wait_ge(step["x2"], g)
                    apart(dve)
                    x2t = lambda i: proj[:, bass.ds(t0 + i, 1), C:2 * C].rearrange("p t c -> p (t c)")
                    stats_c(3, "d", x2t, g - 1)
                if two:
                    dve.wait_ge(step["r_d"], g)
                    dve.wait_ge(step["rows"], g)
                    for i in range(GT):
                        s1 = nc.vector.tensor_scalar(xr4[:, i, :], x2t(i), ln[:, 3, i, 6:7], ln[:, 3, i, 9:10], ALU.subtract, ALU.mult)
                    s1.then_inc(step["xr"], 1)
                    dve.wait_ge(step["lg_ps"], g)
                    nc.vector.tensor_copy(lg[:, bass.ds(t0, GT), :], ps[:, 7, 0:GT * NE].rearrange("p (t e) -> p t e", t=GT)).then_inc(step["lg"], 1)

            c_loop(dve, c_body)

            steps = [0]

            def own(ins):
                steps[0] += 1
                ins.then_inc(rsem["d"], 1)
                dve.wait_ge(rsem["d"], steps[0])

            def over_e(v):
                return v.unsqueeze(2).to_broadcast([P, NT, NE])

            dve.wait_ge(step["lg"], NG)
            own(nc.vector.tensor_reduce(rs[:, 0, :], lg[:, :, :], AX_X, ALU.max))
            nc.vector.tensor_tensor(rt[:, 1, :, :], lg[:, :, :], over_e(rs[:, 0, :]), ALU.subtract).then_inc(rsem["e"], 1)
            own(nc.vector.tensor_tensor(rt[:, 2, :, :], lg[:, :, :], over_e(rs[:, 0, :]), ALU.is_equal))
            own(nc.vector.tensor_tensor(rt[:, 2, :, :], rt[:, 2, :, :], pref[:, :].unsqueeze(1).to_broadcast([P, NT, NE]), ALU.mult))
            own(nc.vector.tensor_reduce(rs[:, 1, :], rt[:, 2, :, :], AX_X, ALU.max))
            nc.vector.tensor_tensor(rt[:, 0, :, :], rt[:, 2, :, :], over_e(rs[:, 1, :]), ALU.is_equal).then_inc(rsem["p"], 1)
            dve.wait_ge(rsem["p"], 2)
            own(nc.vector.tensor_copy(rt[:, 3, :, :], ps[:, 1, 0:NT * NE].rearrange("p (t e) -> p t e", t=NT)))
            for e in range(NE):
                sc = nc.vector.tensor_tensor_scan(rt[:, 4, :, e], ones[:, 0:NT], rt[:, 3, :, e], 0.0, ALU.mult, ALU.add)
            own(sc)
            cnt, til, end, beg = (rs[:, 2 + i, 0:NE] for i in range(4))
            own(nc.vector.tensor_scalar(cnt, rt[:, 4, NT - 1, :], 1.0 / TS, (TS - 1) / (2.0 * TS), ALU.mult, ALU.add))
            own(nc.vector.tensor_scalar(til, cnt, MAGIC, None, ALU.add))
            own(nc.vector.tensor_scalar(til, til, -MAGIC, None, ALU.add))
            own(nc.vector.tensor_tensor_scan(end, ones[:, 0:NE], til, 0.0, ALU.mult, ALU.add))
            own(nc.vector.tensor_tensor(beg, end, til, ALU.subtract))
            own(nc.vector.tensor_tensor(rt[:, 4, :, :], rt[:, 4, :, :], rt[:, 3, :, :], ALU.subtract))
            own(nc.vector.tensor_tensor(rt[:, 4, :, :], rt[:, 4, :, :], ps[:, 0, 0:NT * NE].rearrange("p (t e) -> p t e", t=NT), ALU.add))
            own(nc.vector.scalar_tensor_tensor(rt[:, 4, :, :], beg.unsqueeze(1).to_broadcast([P, NT, NE]), float(TS), rt[:, 4, :, :],
                                               ALU.mult, ALU.add))
            own(nc.vector.tensor_tensor(rt[:, 4, :, :], rt[:, 4, :, :], rt[:, 0, :, :], ALU.mult))
            own(nc.vector.tensor_reduce(rs[:, 6, :], rt[:, 4, :, :], AX_X, ALU.add))
            te = rt[:, 5, 0:NS, :]
            own(nc.vector.tensor_tensor(te, tile_no[:, :].unsqueeze(2).to_broadcast([P, NS, NE]),
                                        end.unsqueeze(1).to_broadcast([P, NS, NE]), ALU.is_ge))
            own(nc.vector.tensor_reduce(rs[:, 7, 0:NS], te, AX_X, ALU.add))
            nc.vector.tensor_scalar(exp_i[:, :], rs[:, 7, 0:NS], NE - 1.0, None, ALU.min).then_inc(rsem["x"], 1)
            dve.wait_ge(rsem["s"], 1)
            own(nc.vector.tensor_reduce(rs[:, 0, :], rt[:, 1, :, :], AX_X, ALU.add))
            nc.vector.reciprocal(proj[:, :, 2 * C], rs[:, 0, :])
            nc.vector.tensor_copy(sl_i[:, :], rs[:, 6, :]).then_inc(rsem["i"], 1)
            own(nc.vector.tensor_scalar(rs[:, 7, 0:NS], rs[:, 7, 0:NS], NE - 1.0, None, ALU.min))
            own(nc.vector.tensor_tensor(te, rs[:, 7, 0:NS].unsqueeze(2).to_broadcast([P, NS, NE]),
                                        pref[:, :].unsqueeze(1).to_broadcast([P, NS, NE]), ALU.add))
            own(nc.vector.tensor_scalar(te, te, float(NE), None, ALU.is_equal))
            for e in range(NE):
                to = fpart if e else fbias
                by = te[:, :, e:e + 1]
                nc.vector.tensor_tensor(to[:, :, 0:EC], eb1_sb[:, e:e + 1, :].to_broadcast([P, NS, EC]),
                                        by.to_broadcast([P, NS, EC]), ALU.mult)
                own(nc.vector.tensor_tensor(to[:, :, EC:EC + 1], eb2_sb[:, e:e + 1].unsqueeze(1).to_broadcast([P, NS, 1]), by, ALU.mult))
                if e:
                    own(nc.vector.tensor_tensor(fbias[:, :, :], fbias[:, :, :], fpart[:, :, :], ALU.add))
            nc.vector.sem_inc(fs["bias"], 1)

            def f_weigh(i, j):
                s = DEPTH * i + j
                par = j % 2
                dve.wait_ge(fs["y_tr"], s + 1)
                if exists(*after(i, j, -2)):
                    dve.wait_ge(fs["res"], s - 1)
                for t in range(RS):
                    wy = nc.vector.tensor_scalar(fwy[par][:, t, :], ps[:, 6, t * P:(t + 1) * P], frow[j][:, t, 2 * C:2 * C + 1],
                                                 None, ALU.mult)
                wy.then_inc(fs["wy"], 1)
                if exists(i - 1, j):
                    dve.wait_ge(f_out[j], 16 * RS * i)
                nc.vector.tensor_scalar(fidx_f[:, j, :], frow[j][:, :, 2 * C + 1], 0.0, 2.0 * NT * P, ALU.is_equal, ALU.mult).then_inc(fs["idxa"], 1)
                dve.wait_ge(fs["wy"], s + 1)
                for t in range(RS):
                    st = nc.vector.bn_stats(fst[:, par, t, 0:6], fwy[par][:, t, :])
                st.then_inc(fs["st"], 1)
                dve.wait_ge(fs["idxa"], s + 1)
                nc.vector.scalar_tensor_tensor(fidx[:, j, :], fidx_f[:, j, :], -1.0, frow[j][:, :, 2 * C + 1], ALU.add, ALU.add).then_inc(fs["idx"], 1)
                dve.wait_ge(fs["st"], s + 1)
                apart(dve)
                for t in range(RS):
                    ag = nc.vector.bn_aggr(fst[:, par, t, 6:8], fst[:, par, t, 0:6])
                ag.then_inc(fs["var"], 1)

            def f_finish(i, j):
                s = DEPTH * i + j
                par = j % 2
                dve.wait_ge(fs["r"], s + 1)
                for t in range(RS):
                    nr = nc.vector.tensor_scalar(fwy[par][:, t, :], fwy[par][:, t, :], fst[:, par, t, 6:7], fst[:, par, t, 9:10],
                                                 ALU.subtract, ALU.mult)
                nr.then_inc(fs["nrm"], 1)
                dve.wait_ge(fs["nrm"], s + 1)
                nc.vector.tensor_tensor(fres[j][:, :, :], fwy[par][:, :, :], frow[j][:, :, C:2 * C], ALU.add).then_inc(fs["res"], 1)

            def f_body(i, j):
                f_weigh(i, j)
                if exists(*after(i, j, -1)):
                    f_finish(*after(i, j, -1))

            f_loop(dve, f_body)
            f_finish(NS // DEPTH - 1, DEPTH - 1)


_INS = ['L0_attn_x', 'L0_attn_Wq', 'L0_attn_bq', 'L0_attn_Wk', 'L0_attn_bk', 'L0_attn_Wv', 'L0_attn_bv',
        'L0_attn_Wc2q', 'L0_attn_bc2q', 'L0_attn_Wo', 'L0_attn_bo', 'L0_attn_g1', 'L0_attn_beta1',
        'L0_attn_g2', 'L0_attn_beta2', 'L0_attn_W1', 'L0_attn_b1', 'L0_attn_Wm', 'L0_attn_bm',
        'L0_attn_Wqo', 'L0_attn_bqo', 'L0_attn_W2', 'L0_attn_b2', 'L0_ffn_gate_w', 'L0_ffn_w1',
        'L0_ffn_b1', 'L0_ffn_w2', 'L0_ffn_b2']
_OUTS = [((16, 256, 128), 'float32')]


def kernel(**inputs):
    import numpy as _np
    import concourse.bacc as _bacc
    from concourse import mybir as _mybir
    from concourse.bass_utils import run_bass_kernel_spmd as _run

    nc = _bacc.Bacc("TRN2", target_bir_lowering=False, num_devices=1)
    arrays, args = {}, []
    for name in _INS:
        a = _np.ascontiguousarray(inputs[name])
        arrays[f"in_{name}_dram"] = a
        args.append(nc.dram_tensor(f"in_{name}_dram", a.shape, _mybir.dt.from_np(a.dtype), kind="ExternalInput").ap())
    for i, (shape, dtype) in enumerate(_OUTS):
        dt = _mybir.dt.from_np(_np.dtype(dtype))
        args.append(nc.dram_tensor(f"out_{i}_dram", shape, dt, kind="ExternalOutput").ap())
    bass_sandwich(nc, *args)
    r = _run(nc, [arrays], core_ids=[0])
    got = tuple(r.results[0][f"out_{i}_dram"] for i in range(len(_OUTS)))
    return got[0]
```
